# Optimizing a Trainium2 kernel written in Bass

```python
import numpy as np
import jax
import jax.numpy as jnp

def _softmax(x, axis=-1):
    return jax.nn.softmax(x, axis=axis)

def _gelu(x):
    return jax.nn.gelu(x, approximate=True)

def _silu(x):
    return jax.nn.silu(x)

def _sigmoid(x):
    return jax.nn.sigmoid(x)

def _layernorm(x, axis=-1, eps=1e-05):
    m = jnp.mean(x, axis=axis, keepdims=True)
    v = jnp.var(x, axis=axis, keepdims=True)
    return (x - m) / jnp.sqrt(v + eps)

def _scatter_add(tgt, idx, src, axis=0):
    return tgt.at[idx].add(src)

def _segment_sum(src, seg, n):
    return jax.ops.segment_sum(src, seg, n)
kernel_name = 'mk_adj_ffn_d1_adj_r2_08409b'

def setup_inputs(seed: int=0):
    np.random.seed(seed)
    _w = jnp.asarray

    def _rec_inputs():
        import jax
        import jax.numpy as jnp
        _gk = jax.random.key(seed)
        x = -0.0005207 + 1.001 * jax.random.normal(jax.random.fold_in(_gk, 1), (4096, 128), jnp.float32)
        _w = (1.0 + jnp.arange(4096, dtype=jnp.float32)) ** (-0.5)
        _w = _w / _w.mean()
        _pij = jnp.clip(0.00390625 * _w[:, None] * _w[None, :], 0.0, 1.0)
        _a = jax.random.uniform(jax.random.fold_in(_gk, 2), (4096, 4096)) < _pij
        adj = _a.astype(jnp.int32)
        return (x, adj)
    x, adj = _rec_inputs()

    def _L0_gnn_setup():
        import jax, jax.numpy as jnp
        import numpy as np
        SIZE_U = 2048
        SIZE_V = 2048
        N = SIZE_U + SIZE_V
        D_IN = 128
        QK_DIM = 128
        V_DIM = 128
        HEADS = 2
        DH = QK_DIM // HEADS
        DV = V_DIM // HEADS
        SCALE = DH ** (-0.5)
        NEG_INF = -9000000000000000.0
        key = jax.random.key(seed)
        ks = jax.random.split(key, 8)
        s = 1.0 / np.sqrt(D_IN)
        x = jax.random.normal(ks[0], (N, D_IN), jnp.float32)
        adj = jax.random.randint(ks[1], (N, N), 0, 2, jnp.int32)
        Wq = jax.random.normal(ks[2], (D_IN, QK_DIM), jnp.float32) * s
        Wk = jax.random.normal(ks[3], (D_IN, QK_DIM), jnp.float32) * s
        Wv = jax.random.normal(ks[4], (D_IN, V_DIM), jnp.float32) * s
        weightr = jax.random.normal(ks[5], (V_DIM, V_DIM), jnp.float32) * s
        weightd = jax.random.normal(ks[6], (V_DIM, V_DIM), jnp.float32) * s
        bias = jnp.zeros((V_DIM,), jnp.float32)
        return {'x': x, 'adj': adj, 'Wq': Wq, 'Wk': Wk, 'Wv': Wv, 'weightr': weightr, 'weightd': weightd, 'bias': bias}
    _L0_gnn_all = _L0_gnn_setup()
    _L0_gnn_in = {k: v for k, v in _L0_gnn_all.items() if k in ('Wq', 'Wk', 'Wv', 'weightr', 'weightd', 'bias')}
    del _L0_gnn_all

    def _L0_ffn_setup():
        import jax, jax.numpy as jnp
        import numpy as np
        B, S, D, E, H, K = (4, 2048, 128, 8, 256, 2)
        key = jax.random.key(seed)
        ks = jax.random.split(key, 6)
        x = jax.random.normal(ks[0], (B, S, D), jnp.float32)
        Wg = jax.random.normal(ks[1], (D, E), jnp.float32) * 0.02
        bg = jnp.zeros((E,), jnp.float32)
        W1 = jax.random.normal(ks[2], (E, D, H), jnp.float32) * 0.02
        b1 = jnp.zeros((E, H), jnp.float32)
        W2 = jax.random.normal(ks[3], (E, H, D), jnp.float32) * 0.02
        b2 = jnp.zeros((E, D), jnp.float32)
        return {'x': x, 'Wg': Wg, 'bg': bg, 'W1': W1, 'b1': b1, 'W2': W2, 'b2': b2}
    _L0_ffn_all = _L0_ffn_setup()
    _L0_ffn_in = {k: v for k, v in _L0_ffn_all.items() if k in ('Wg', 'bg', 'W1', 'b1', 'W2', 'b2')}
    del _L0_ffn_all
    return {'x': x, 'adj': adj, 'L0_gnn_Wq': _L0_gnn_in['Wq'], 'L0_gnn_Wk': _L0_gnn_in['Wk'], 'L0_gnn_Wv': _L0_gnn_in['Wv'], 'L0_gnn_weightr': _L0_gnn_in['weightr'], 'L0_gnn_weightd': _L0_gnn_in['weightd'], 'L0_gnn_bias': _L0_gnn_in['bias'], 'L0_ffn_Wg': _L0_ffn_in['Wg'], 'L0_ffn_bg': _L0_ffn_in['bg'], 'L0_ffn_W1': _L0_ffn_in['W1'], 'L0_ffn_b1': _L0_ffn_in['b1'], 'L0_ffn_W2': _L0_ffn_in['W2'], 'L0_ffn_b2': _L0_ffn_in['b2']}

def reference(x, adj, L0_gnn_Wq, L0_gnn_Wk, L0_gnn_Wv, L0_gnn_weightr, L0_gnn_weightd, L0_gnn_bias, L0_ffn_Wg, L0_ffn_bg, L0_ffn_W1, L0_ffn_b1, L0_ffn_W2, L0_ffn_b2):
    import jax
    import jax.numpy as jnp

    def _L0_gnn_ref(x, adj, Wq, Wk, Wv, weightr, weightd, bias):
        import jax, jax.numpy as jnp
        import numpy as np
        SIZE_U = 2048
        SIZE_V = 2048
        N = SIZE_U + SIZE_V
        D_IN = 128
        QK_DIM = 128
        V_DIM = 128
        HEADS = 2
        DH = QK_DIM // HEADS
        DV = V_DIM // HEADS
        SCALE = DH ** (-0.5)
        NEG_INF = -9000000000000000.0
        q = (x @ Wq).reshape(N, HEADS, DH)
        k = (x @ Wk).reshape(N, HEADS, DH)
        v = (x @ Wv).reshape(N, HEADS, DV)
        scores = jnp.einsum('nhd,mhd->hnm', q * SCALE, k)
        scores = jnp.where(adj[None, :, :] > 0, scores, NEG_INF)
        attn = jax.nn.softmax(scores, axis=-1)
        sat = jnp.einsum('hnm,mhd->nhd', attn, v).reshape(N, V_DIM)
        out = jnp.concatenate([sat[:SIZE_U] @ weightr, sat[SIZE_U:] @ weightd], axis=0)
        out = out + bias
        return jax.nn.leaky_relu(out, negative_slope=0.01)

    def _L0_ffn_ref(x, Wg, bg, W1, b1, W2, b2):
        import jax, jax.numpy as jnp
        import numpy as np
        B, S, D, E, H, K = (4, 2048, 128, 8, 256, 2)
        Bv, Sv, Dv = x.shape
        gate_scores = x @ Wg + bg
        _, idx = jax.lax.top_k(gate_scores, K)
        mask = jax.nn.one_hot(idx, E, dtype=x.dtype).sum(axis=-2)
        xf = x.reshape(-1, Dv)
        mf = mask.reshape(-1, E)
        h = jax.nn.gelu(jnp.einsum('td,edh->teh', xf, W1) + b1[None], approximate=False)
        y = jnp.einsum('teh,ehd->ted', h, W2) + b2[None]
        out = jnp.einsum('ted,te->td', y, mf)
        return out.reshape(Bv, Sv, Dv)
    x = x + _L0_gnn_ref(_layernorm(x, axis=-1), adj, L0_gnn_Wq, L0_gnn_Wk, L0_gnn_Wv, L0_gnn_weightr, L0_gnn_weightd, L0_gnn_bias)
    x = x + _L0_ffn_ref(_layernorm(x, axis=-1)[None], L0_ffn_Wg, L0_ffn_bg, L0_ffn_W1, L0_ffn_b1, L0_ffn_W2, L0_ffn_b2)[0]
    return x

_drawn_inputs = setup_inputs


def setup_inputs(seed=0):
    import zlib

    import numpy as np

    out = dict(_drawn_inputs(seed))
    spreads = {'L0_gnn_bias': (0.0, 0.1),
     'L0_ffn_bg': (0.0, 0.1),
     'L0_ffn_b1': (0.0, 0.357),
     'L0_ffn_b2': (0.0, 0.1)}
    factors = {}
    for name, (base, spread) in spreads.items():
        noise = np.random.default_rng([zlib.crc32(name.encode()), seed]).standard_normal(out[name].shape)
        drawn = base * np.exp(spread * noise) if base else spread * noise
        out[name] = jnp.asarray(drawn.astype(out[name].dtype))
    for name, factor in factors.items():
        out[name] = (out[name] * factor).astype(out[name].dtype)
    return out
```

```python
from contextlib import ExitStack

import concourse.bass as bass
from concourse import mybir

F32 = mybir.dt.float32
F16 = mybir.dt.float16
BF16 = mybir.dt.bfloat16
I32 = mybir.dt.int32
ALU = mybir.AluOpType
ACT = mybir.ActivationFunctionType
AX_X = mybir.AxisListType.X

P = 128
N, D = 4096, 128
HEADS = 2
DH = D // HEADS
SCALE = float(DH) ** -0.5
EPS = 1e-5
SLOPE = 0.01
BIG = 2.0 ** 64
NT = N // P
CH = 512
NC = N // CH
TPC = CH // P
DV1 = DH + 1
E, H, HB = 8, 256, 2
HALF = N // 2
PIECES = 4
PIECE = N // PIECES

SCORE_BANKS = 4
TR0, AV0 = 4, 6
PT_RING = 4
LAG = 3
DVE_COPIES = (3, 7)
ACT_COPIES = tuple(g for g in range(NC) if g not in DVE_COPIES)


def build(nc, x, adj, wq, wk, wv, wr, wd, bias, wg, bg, w1, b1, w2, b2, out):
    with ExitStack() as ctx:
        def sb(name, shape, dt):
            return ctx.enter_context(nc.sbuf_tensor(name, shape, dt))

        def sem(name):
            return ctx.enter_context(nc.semaphore(name))

        ident = sb("ident", [P, P], F32)
        x_sb = sb("x_sb", [P, NT, D], F32)
        adj_raw = sb("adj_raw", [P, 2, HALF], I32)
        mask = sb("mask", [P, 2, N], BF16)
        neg_s = sb("neg_s", [P, HEADS, N], F32)
        prob = sb("prob", [P, HEADS, N], F32)
        prob_t = sb("prob_t", [P, PT_RING, CH], F32)
        q_pair = sb("q_pair", [P, HEADS, N], F16)
        k_pair = sb("k_pair", [P, HEADS, N], F16)
        k_swap = sb("k_swap", [P, HEADS, N], F16)
        v_sb = sb("v_sb", [P, NT, HEADS, DV1], F32)
        wq2 = sb("wq2", [P, HEADS, 2, DH], F32)
        wk2 = sb("wk2", [P, HEADS, 2, DH], F32)
        wv_sb = sb("wv_sb", [P, D], F32)
        wrd = sb("wrd", [P, 2, D], F32)
        bias_b = sb("bias_b", [P, D], F32)
        wg_sb = sb("wg_sb", [P, E], F32)
        bg_b = sb("bg_b", [P, E], F32)
        b1_sb = sb("b1_sb", [P, E, HB], F32)
        b2_sb = sb("b2_sb", [E, D], F32)
        stats = sb("stats", [P, 8, 6], F32)
        mv = sb("mv", [P, NT, 2], F32)
        ve = sb("ve", [P, NT], F32)
        rstd = sb("rstd", [P, NT], F32)
        nwt = sb("nwt", [P, NT], F32)
        low = sb("low", [P, HEADS, NC], F32)
        nmax = sb("nmax", [P, HEADS], F32)
        rsum = sb("rsum", [P, HEADS], F32)
        sat = sb("sat", [P, D], F32)
        sat_t = sb("sat_t", [P, D], F32)
        o_pre = sb("o_pre", [P, D], F32)
        o_act = sb("o_act", [P, D], F32)
        mv_tile = sb("mv_tile", [P, 2], F32)

        xn = prob[:, 0, 0:2 * CH].rearrange("p (r t d) -> p r t d", r=2, t=TPC)
        xn_t = prob[:, 1, 0:2 * CH].rearrange("p (r c) -> p r c", r=2)
        w1_sb = adj_raw[:, 0, :].bitcast(F32).rearrange("p (e h) -> p e h", e=E)
        w2_sb = adj_raw[:, 1, :].bitcast(F32).rearrange("p (e b d) -> p e b d", e=E, b=HB)
        x2 = prob[:, 0, 0:2 * CH].rearrange("p (r t d) -> p r t d", r=2, t=TPC)
        x2_t = prob[:, 1, 0:2 * CH].rearrange("p (r c) -> p r c", r=2)
        hid = neg_s[:, 0, 0:4 * CH].rearrange("p (r c) -> p r c", r=4)
        acc = neg_s[:, 1, 0:2 * CH].rearrange("p (r t d) -> p r t d", r=2, t=TPC)
        gbase = neg_s[:, 1, 2 * CH:2 * CH + 512]
        logit = gbase[:, 0:32].rearrange("p (t e) -> p t e", e=E)
        top8 = gbase[:, 32:64].rearrange("p (t e) -> p t e", e=E)
        above = gbase[:, 64:96].rearrange("p (t e) -> p t e", e=E)
        tied = gbase[:, 96:128].rearrange("p (t e) -> p t e", e=E)
        rank = gbase[:, 128:160].rearrange("p (t e) -> p t e", e=E)
        keep = gbase[:, 160:192].rearrange("p (t e) -> p t e", e=E)
        gate = gbase[:, 192:256].rearrange("p (r t e) -> p r t e", r=2, e=E)
        gate_t = neg_s[0:E, 1, 4 * CH:5 * CH]

        ps = ctx.enter_context(nc.psum_tensor("ps", [P, 8, CH], F32))

        x_in = [sem(f"x_in{i}") for i in range(4)]
        w_in = sem("w_in")
        ffn_w_in = sem("ffn_w_in")
        adj_in = [sem(f"adj_in{q}") for q in range(2)]
        swap_in = sem("swap_in")
        out_done = [sem(f"out_done{r}") for r in range(2)]
        ident_zero = sem("ident_zero")
        ident_ready = sem("ident_ready")
        ones_ready = sem("ones_ready")
        clamped = sem("clamped")
        mask_ready = sem("mask_ready")
        stats_chain = sem("stats_chain")
        rstd_chain = sem("rstd_chain")
        sqrt_done = sem("sqrt_done")
        xn_ready = sem("xn_ready")
        xnt_psum = sem("xnt_psum")
        xnt_ready = sem("xnt_ready")
        proj_psum = sem("proj_psum")
        hi_ready = sem("hi_ready")
        lo_ready = sem("lo_ready")
        v_psum = sem("v_psum")
        v_ready = sem("v_ready")
        scores_ready = sem("scores_ready")
        masked = sem("masked")
        max_ready = sem("max_ready")
        exp_done = sem("exp_done")
        transposed = sem("transposed")
        pt_by_act = sem("pt_by_act")
        pt_by_dve = sem("pt_by_dve")
        av_done = sem("av_done")
        sum_inv = sem("sum_inv")
        sat_ready = sem("sat_ready")
        satt_psum = sem("satt_psum")
        satt_ready = sem("satt_ready")
        o_psum = sem("o_psum")
        o_read = sem("o_read")
        post_chain = sem("post_chain")
        x2_ready = sem("x2_ready")
        x2t_psum = sem("x2t_psum")
        x2t_ready = sem("x2t_ready")
        logit_psum = sem("logit_psum")
        gate_chain = sem("gate_chain")
        gate_ready = sem("gate_ready")
        gatet_psum = sem("gatet_psum")
        gatet_ready = sem("gatet_ready")
        b2_psum = sem("b2_psum")
        acc_ready = sem("acc_ready")
        up_done = sem("up_done")
        hid_ready = sem("hid_ready")
        down_done = sem("down_done")
        combined = sem("combined")

        def pairs(eng, first, end, body):
            with eng.Fori(0, (end - first) // 2) as k:
                body(2 * k + first, first % 2)
                body(2 * k + first + 1, (first + 1) % 2)

        def wait_pt(eng, unit, g):
            if g in DVE_COPIES:
                eng.wait_ge(pt_by_dve, len(DVE_COPIES) * unit + DVE_COPIES.index(g) + 1)
            else:
                eng.wait_ge(pt_by_act, len(ACT_COPIES) * unit + ACT_COPIES.index(g) + 1)

        block = ctx.enter_context(nc.Block())
        N_W = 11

        @block.sync
        def _(sp):
            xv = x.rearrange("(t p) d -> p t d", p=P)
            for i in range(4):
                t = NT // 4
                sp.dma_start(x_sb[:, i * t:(i + 1) * t, :], xv[:, i * t:(i + 1) * t, :]).then_inc(x_in[i], 16)

            def load_adj(i):
                for q in range(2):
                    if not isinstance(i, int) or i > 0:
                        sp.wait_ge(clamped, 2 * (i - 1) + q + 1)
                    sp.dma_start(adj_raw[:, q, :], adj[bass.ds(i * P, P), q * HALF:(q + 1) * HALF]).then_inc(adj_in[q], 16)

            load_adj(0)
            load_adj(1)
            for c in range(2):
                sp.wait_ge(lo_ready, 4 * (c + 1) * (NC // 2))
                sp.wait_ge(hi_ready, 4 * (c + 1) * (NC // 2))
                cols = slice(c * HALF, (c + 1) * HALF)
                for h in range(HEADS):
                    sp.dma_start(k_swap[0:DH, h, cols], k_pair[DH:P, h, cols]).then_inc(swap_in, 16)
                    sp.dma_start(k_swap[DH:P, h, cols], k_pair[0:DH, h, cols]).then_inc(swap_in, 16)
            pairs(sp, 2, NT, lambda i, par: load_adj(i))
            sp.wait_ge(clamped, 2 * NT)
            sp.dma_start(w1_sb, w1.rearrange("e d h -> d e h")).then_inc(ffn_w_in, 16)
            sp.dma_start(w2_sb, w2.rearrange("e (b p) d -> p e b d", b=HB)).then_inc(ffn_w_in, 16)

            ov = out.rearrange("(t p) d -> p t d", p=P)

            def store(j, par):
                sp.wait_ge(combined, E * j + E)
                sp.dma_start(ov[:, bass.ds(j * TPC, TPC), :], acc[:, par]).then_inc(out_done[par], 16)

            pairs(sp, 0, NC, store)
            for r in range(2):
                sp.wait_ge(out_done[r], 16 * NC // 2)

        @block.gpsimd
        def _(pool):
            pool.memset(ident[:, :], 0.0).then_inc(ident_zero, 1)
            pool.wait_ge(ident_zero, 1)
            pool.affine_select(out=ident[:, :], in_=ident[:, :], compare_op=ALU.not_equal, fill=1.0, base=0,
                               pattern=[[-1, P]], channel_multiplier=1).then_inc(ident_ready, 1)
            pool.memset(v_sb[:, :, :, DH:DV1], 1.0).then_inc(ones_ready, 1)

            def make_mask(i, par):
                for q in range(2):
                    half = mask[:, par, q * HALF:(q + 1) * HALF]
                    pool.wait_ge(adj_in[q], 16 * (i + 1))
                    if not isinstance(i, int) or i >= 2:
                        pool.wait_ge(masked, 16 * (i - 2) + 16)
                    pool.nop(nofuse=True)
                    pool.tensor_scalar(half, adj_raw[:, q, :], 1.0, 0.0, ALU.min, ALU.max).then_inc(clamped, 1)
                for q in range(2):
                    half = mask[:, par, q * HALF:(q + 1) * HALF]
                    pool.wait_ge(clamped, 2 * i + q + 1)
                    pool.nop(nofuse=True)
                    pool.tensor_scalar(half, half, BIG, -BIG, ALU.mult, ALU.add).then_inc(mask_ready, 1)

            make_mask(0, 0)
            make_mask(1, 1)
            pairs(pool, 2, NT, make_mask)

        @block.scalar
        def _(act):
            act.dma_start(wq2[:, :, 0, :], wq.rearrange("d (h c) -> d h c", h=HEADS)).then_inc(w_in, 16)
            act.dma_start(wq2[:, :, 1, :], wq.rearrange("d (h c) -> d h c", h=HEADS)).then_inc(w_in, 16)
            act.dma_start(wk2[:, :, 0, :], wk.rearrange("d (h c) -> d h c", h=HEADS)).then_inc(w_in, 16)
            act.dma_start(wk2[:, :, 1, :], wk.rearrange("d (h c) -> d h c", h=HEADS)).then_inc(w_in, 16)
            act.dma_start(wv_sb[:, :], wv).then_inc(w_in, 16)
            act.dma_start(wrd[:, 0, :], wr).then_inc(w_in, 16)
            act.dma_start(wrd[:, 1, :], wd).then_inc(w_in, 16)
            act.dma_start(bias_b[:, :], bias.rearrange("(a d) -> a d", a=1).to_broadcast([P, D])).then_inc(w_in, 16)
            act.dma_start(wg_sb[:, :], wg).then_inc(w_in, 16)
            act.dma_start(bg_b[:, :], bg.rearrange("(a d) -> a d", a=1).to_broadcast([P, E])).then_inc(w_in, 16)
            act.dma_start(b2_sb[:, :], b2).then_inc(w_in, 16)
            with nc.allow_non_contiguous_dma(reason="2048 values, once"):
                act.dma_start(b1_sb[:, :, :], b1.rearrange("e (b p) -> p e b", p=P)).then_inc(ffn_w_in, 16)

            act.wait_ge(rstd_chain, 1)
            act.activation(rstd[:, :], ve[:, :], ACT.Sqrt).then_inc(sqrt_done, 1)

            def project(j, par):
                cols = bass.ds(j * CH, CH)
                act.wait_ge(xnt_psum, j + 1)
                if not isinstance(j, int) or j >= 2:
                    act.wait_ge(v_psum, j - 1)
                act.activation(xn_t[:, par, :], ps[:, TR0 + par, :], ACT.Copy).then_inc(xnt_ready, 1)
                for m, (dst, scale) in enumerate(((q_pair, SCALE), (k_pair, 1.0))):
                    for h in range(HEADS):
                        act.wait_ge(proj_psum, 4 * j + 2 * m + h + 1)
                        act.activation(dst[:, h, cols], ps[:, 2 * m + h, :], ACT.Copy, scale=scale).then_inc(hi_ready, 1)

            project(0, 0)
            project(1, 1)
            pairs(act, 2, NC, project)

            def exp_piece(j, h, n, first=False):
                if n == 0:
                    act.wait_ge(max_ready, 2 * j + h + 1)
                    if not first:
                        act.wait_ge(transposed, 16 * (j - 1) + 8 * h + 8)
                cols = slice(n * PIECE, (n + 1) * PIECE)
                act.activation(prob[:, h, cols], neg_s[:, h, cols], ACT.Exp, bias=nmax[:, h:h + 1],
                               scale=-1.0).then_inc(exp_done, 1)

            def copy_pt(j, h, g, early=False):
                act.wait_ge(transposed, 16 * j + 8 * h + g + 1)
                if not (early and h == 0 and g < PT_RING):
                    act.wait_ge(av_done, 16 * j + 8 * h + g - PT_RING + 1)
                act.activation(prob_t[:, g % PT_RING, :], ps[:, TR0 + g % 2, :], ACT.Copy).then_inc(pt_by_act, 1)

            def step(i, prior=True, now=True, post=True, early=False):
                for h in range(HEADS):
                    has_exp = prior if h == 0 else now
                    ej, eh = (i - 1, 1) if h == 0 else (i, 0)
                    first = (isinstance(i, int) and ((i <= 1 and h == 0) or i == 0))
                    for n in range(PIECES):
                        if has_exp:
                            exp_piece(ej, eh, n, first)
                        if prior:
                            for g in (2 * n, 2 * n + 1):
                                if g in ACT_COPIES:
                                    copy_pt(i - 1, h, g, early)
                        if post and h == 0 and n == 2:
                            act.wait_ge(satt_psum, i - 1)
                            act.activation(sat_t[:, :], ps[:, AV0 + 1, P:2 * P], ACT.Copy).then_inc(satt_ready, 1)

            step(0, prior=False, post=False)
            step(1, post=False, early=True)
            pairs(act, 2, NT, lambda i, par: step(i))
            step(NT, now=False)
            act.wait_ge(satt_psum, NT)
            act.activation(sat_t[:, :], ps[:, AV0 + 1, P:2 * P], ACT.Copy).then_inc(satt_ready, 1)

            act.wait_ge(rstd_chain, 7)
            act.activation(rstd[:, :], ve[:, :], ACT.Sqrt).then_inc(sqrt_done, 1)
            act.wait_ge(ffn_w_in, 48)

            def x2t_copy(j, par):
                act.wait_ge(x2t_psum, j + 1)
                act.activation(x2_t[:, par, :], ps[:, TR0, :], ACT.Copy).then_inc(x2t_ready, 1)

            def gatet_copy(j):
                act.wait_ge(gatet_psum, j + 1)
                act.activation(gate_t, ps[0:E, TR0 + 1, :], ACT.Copy).then_inc(gatet_ready, 1)

            def ffn(j, par, prep=True, early=False):
                for e in range(E):
                    for b in range(HB):
                        f = 16 * j + 2 * e + b
                        act.wait_ge(up_done, f + 1)
                        if not (early and e < 2):
                            act.wait_ge(down_done, 8 * j + e - 1)
                        act.activation(hid[:, (2 * e + b) % 4, :], ps[:, (2 * e + b) % 4, :], ACT.Gelu,
                                       bias=b1_sb[:, e, b:b + 1]).then_inc(hid_ready, 1)
                    if prep and e == 1:
                        x2t_copy(j + 1, 1 - par)
                    if prep and e == 5:
                        gatet_copy(j + 1)

            x2t_copy(0, 0)
            gatet_copy(0)
            ffn(0, 0, early=True)
            ffn(1, 1)
            pairs(act, 2, NC - 2, ffn)
            ffn(NC - 2, 0)
            ffn(NC - 1, 1, prep=False)

        @block.vector
        def _(dve):
            def linker(s, base):
                count = [base]

                def link(ins):
                    count[0] = count[0] + 1
                    ins.then_inc(s, 1)
                    dve.wait_ge(s, count[0])
                return link

            def settled():
                dve.nop(nofuse=True)

            def inverse_std(n):
                link = linker(rstd_chain, 6 * n)
                link(dve.tensor_scalar(ve[:, :], mv[:, :, 1], EPS, None, ALU.add))
                dve.wait_ge(sqrt_done, n + 1)
                link(dve.reciprocal(rstd[:, :], rstd[:, :]))
                link(dve.tensor_tensor(nwt[:, :], rstd[:, :], rstd[:, :], ALU.mult))
                link(dve.tensor_tensor(nwt[:, :], nwt[:, :], ve[:, :], ALU.mult))
                link(dve.tensor_scalar(nwt[:, :], nwt[:, :], -0.5, 1.5, ALU.mult, ALU.add))
                link(dve.tensor_tensor(rstd[:, :], rstd[:, :], nwt[:, :], ALU.mult))

            for i in range(4):
                dve.wait_ge(x_in[i], 16)
                for t in range(8):
                    ins = dve.bn_stats(stats[:, t, :], x_sb[:, 8 * i + t, :])
                ins.then_inc(stats_chain, 1)
                dve.wait_ge(stats_chain, 2 * i + 1)
                for t in range(8):
                    ins = dve.bn_aggr(mv[:, 8 * i + t, :], stats[:, t, :])
                ins.then_inc(stats_chain, 1)
                dve.wait_ge(stats_chain, 2 * i + 2)
            inverse_std(0)

            def normalise(dst, j, par, done):
                for t in range(TPC):
                    tile = j * TPC + t
                    ins = dve.tensor_scalar(dst[:, par, t, :], x_sb[:, tile, :], mv[:, tile, 0:1],
                                            rstd[:, bass.ds(tile, 1)], ALU.subtract, ALU.mult)
                ins.then_inc(done, 1)

            def project(j, par):
                if not isinstance(j, int) or j >= 2:
                    dve.wait_ge(xnt_psum, j - 1)
                normalise(xn, j, par, xn_ready)
                cols = bass.ds(j * CH, CH)
                for m, (pair, scale) in enumerate(((q_pair, SCALE), (k_pair, 1.0))):
                    for h in range(HEADS):
                        dve.wait_ge(hi_ready, 4 * j + 2 * m + h + 1)
                        lo = pair[DH:P, h, cols]
                        dve.scalar_tensor_tensor(lo, ps[DH:P, 2 * m + h, :], scale, lo, ALU.mult,
                                                 ALU.subtract).then_inc(lo_ready, 1)
                dve.wait_ge(v_psum, j + 1)
                dve.tensor_copy(v_sb[:, bass.ds(j * TPC, TPC), :, 0:DH],
                                ps[:, AV0 + par, :].rearrange("p (t h c) -> p t h c", t=TPC, h=HEADS)).then_inc(v_ready, 1)

            project(0, 0)
            project(1, 1)
            pairs(dve, 2, NC, project)

            def mask_scores(i, par, h, c):
                f = 16 * i + 8 * h + c
                dve.wait_ge(scores_ready, f + 1)
                if c == 0:
                    dve.wait_ge(mask_ready, 2 * i + 2)
                    if not isinstance(i, int) or i >= 1:
                        dve.wait_ge(exp_done, PIECES * (2 * (i - 1) + h + 1))
                cols = slice(c * CH, (c + 1) * CH)
                settled()
                dve.tensor_tensor_reduce(out=neg_s[:, h, cols], in0=ps[:, c % SCORE_BANKS, :], in1=mask[:, par, cols],
                                         scale=-1.0, scalar=3.0e38, op0=ALU.add, op1=ALU.min,
                                         accum_out=low[:, h, c:c + 1]).then_inc(masked, 1)

            def copy_pt(j, h, g, early=False):
                dve.wait_ge(transposed, 16 * j + 8 * h + g + 1)
                if not (early and h == 0 and g < PT_RING):
                    dve.wait_ge(av_done, 16 * j + 8 * h + g - PT_RING + 1)
                dve.tensor_copy(prob_t[:, g % PT_RING, :], ps[:, TR0 + g % 2, :]).then_inc(pt_by_dve, 1)

            def finish_head(j, h):
                dve.wait_ge(av_done, 16 * j + 8 * h + 8)
                dve.reciprocal(rsum[:, h:h + 1], ps[:, AV0 + h, DH:DV1]).then_inc(sum_inv, 1)
                dve.wait_ge(sum_inv, 2 * j + h + 1)
                if not isinstance(j, int) or j >= 1:
                    dve.wait_ge(satt_psum, j)
                dve.tensor_scalar(sat[:, h * DH:(h + 1) * DH], ps[:, AV0 + h, 0:DH], rsum[:, h:h + 1], None,
                                  ALU.mult).then_inc(sat_ready, 1)

            def finish_tile(j):
                dve.wait_ge(o_psum, j + 1)
                dve.tensor_tensor(o_pre[:, :], ps[:, AV0 + 1, 2 * P:3 * P], bias_b[:, :], ALU.add).then_inc(o_read, 1)
                dve.wait_ge(o_read, j + 1)
                link = linker(post_chain, 5 * j)
                link(dve.scalar_tensor_tensor(o_act[:, :], o_pre[:, :], SLOPE, o_pre[:, :], ALU.mult, ALU.max))
                link(dve.tensor_tensor(o_act[:, :], x_sb[:, j, :], o_act[:, :], ALU.add))
                settled()
                dve.tensor_copy(x_sb[:, j, :], o_act[:, :])
                link(dve.bn_stats(stats[:, 0, :], o_act[:, :]))
                settled()
                link(dve.bn_aggr(mv_tile[:, :], stats[:, 0, :]))
                settled()
                link(dve.tensor_copy(mv[:, j, :], mv_tile[:, :]))

            def step(i, par, prior=True, now=True, post=True, early=False):
                for h in range(HEADS):
                    for c in range(NC):
                        if now:
                            mask_scores(i, par, h, c)
                        if prior and c in DVE_COPIES:
                            copy_pt(i - 1, h, c, early)
                        if c == 4 and h == 0 and post:
                            finish_head(i - 2, 1)
                        if c == 4 and h == 1 and prior:
                            finish_head(i - 1, 0)
                        if c == 0 and h == 1 and post:
                            finish_tile(i - 2)
                    if now:
                        dve.wait_ge(masked, 16 * i + 8 * h + 8)
                        dve.tensor_reduce(nmax[:, h:h + 1], low[:, h, :], AX_X, ALU.min).then_inc(max_ready, 1)

            dve.wait_ge(w_in, 16 * N_W)
            step(0, 0, prior=False, post=False)
            step(1, 1, post=False, early=True)
            pairs(dve, 2, NT, step)
            step(NT, 0, now=False)
            finish_head(NT - 1, 1)
            finish_tile(NT - 1)

            inverse_std(1)

            def gates(j, par):
                STEPS = 13
                link = linker(gate_chain, STEPS * j)
                dve.wait_ge(logit_psum, j + 1)
                link(dve.tensor_tensor(logit, ps[:, TR0 + 1, 0:TPC * E].rearrange("p (t e) -> p t e", e=E),
                                       bg_b[:, :].unsqueeze(1).to_broadcast([P, TPC, E]), ALU.add))
                settled()
                for t in range(TPC):
                    link(dve.max(top8[:, t, :], logit[:, t, :])) if t == TPC - 1 else dve.max(top8[:, t, :], logit[:, t, :])
                second = top8[:, :, 1:2].to_broadcast([P, TPC, E])
                dve.tensor_tensor(above, logit, second, ALU.is_gt)
                link(dve.tensor_tensor(tied, logit, second, ALU.is_equal))
                link(dve.tensor_reduce(rank[:, :, 0:1], above, AX_X, ALU.add))
                for e in range(1, E):
                    link(dve.tensor_tensor(rank[:, :, e:e + 1], rank[:, :, e - 1:e], tied[:, :, e - 1:e], ALU.add))
                link(dve.tensor_scalar(keep, rank, 2.0, None, ALU.is_lt))
                link(dve.tensor_tensor(keep, keep, tied, ALU.mult))
                dve.tensor_tensor(gate[:, par], keep, above, ALU.add).then_inc(gate_ready, 1)

            def begin_acc(j, par):
                dve.wait_ge(b2_psum, j + 1)
                if not isinstance(j, int) or j >= 2:
                    dve.wait_ge(out_done[par], 8 * j - 8 * par)
                dve.tensor_tensor(acc[:, par], ps[:, TR0, :].rearrange("p (t d) -> p t d", d=D),
                                  x_sb[:, bass.ds(j * TPC, TPC), :], ALU.add).then_inc(acc_ready, 1)

            def combine(j, par, e):
                dve.wait_ge(down_done, 8 * j + e + 1)
                if e == 0:
                    dve.wait_ge(acc_ready, j + 1)
                else:
                    dve.wait_ge(combined, 8 * j + e)
                for t in range(TPC):
                    ins = dve.scalar_tensor_tensor(acc[:, par, t, :], ps[:, AV0 + e % 2, t * D:(t + 1) * D],
                                                   gate[:, par, t, e:e + 1], acc[:, par, t, :], ALU.mult, ALU.add)
                ins.then_inc(combined, 1)

            def ffn(j, par, prep=True):
                if prep:
                    if not isinstance(j, int) or j >= 1:
                        dve.wait_ge(x2t_psum, j)
                    normalise(x2, j + 1, 1 - par, x2_ready)
                for e in range(E):
                    combine(j, par, e)
                    if prep and e == 2:
                        gates(j + 1, 1 - par)
                    if prep and e == 6:
                        begin_acc(j + 1, 1 - par)

            normalise(x2, 0, 0, x2_ready)
            gates(0, 0)
            begin_acc(0, 0)
            ffn(0, 0)
            ffn(1, 1)
            pairs(dve, 2, NC - 2, ffn)
            ffn(NC - 2, 0)
            ffn(NC - 1, 1, prep=False)

        @block.tensor
        def _(pe):
            pe.wait_ge(ident_ready, 1)
            pe.wait_ge(w_in, 16 * N_W)

            def project(j, par):
                first = isinstance(j, int) and j == 0
                pe.wait_ge(xn_ready, j + 1)
                if not isinstance(j, int) or j >= 2:
                    pe.wait_ge(xnt_ready, j - 1)
                for t in range(TPC):
                    ins = pe.transpose(ps[:, TR0 + par, t * P:(t + 1) * P], xn[:, par, t, :], ident[:, :])
                ins.then_inc(xnt_psum, 1)
                pe.wait_ge(xnt_ready, j + 1)
                for m, w in enumerate((wq2, wk2)):
                    for h in range(HEADS):
                        if not first:
                            pe.wait_ge(lo_ready, 4 * (j - 1) + 2 * m + h + 1)
                        pe.matmul(ps[:, 2 * m + h, :], w[:, h, :, :].rearrange("d r c -> d (r c)"), xn_t[:, par, :],
                                  start=True, stop=True).then_inc(proj_psum, 1)
                if not isinstance(j, int) or j >= 2:
                    pe.wait_ge(v_ready, j - 1)
                for t in range(TPC):
                    ins = pe.matmul(ps[:, AV0 + par, t * P:(t + 1) * P], xn_t[:, par, t * P:(t + 1) * P], wv_sb[:, :],
                                    start=True, stop=True)
                ins.then_inc(v_psum, 1)

            project(0, 0)
            project(1, 1)
            pairs(pe, 2, NC, project)
            pe.wait_ge(lo_ready, 4 * NC)
            pe.wait_ge(v_ready, NC)
            pe.wait_ge(ones_ready, 1)
            pe.wait_ge(swap_in, 16 * 8)

            def scores(i, h, c):
                if not (isinstance(i, int) and i == 0 and h == 0 and c < SCORE_BANKS):
                    pe.wait_ge(masked, 16 * i + 8 * h + c - SCORE_BANKS + 1)
                q = q_pair[:, h, bass.ds(i * P, P)]
                cols = slice(c * CH, (c + 1) * CH)
                bank = ps[:, c % SCORE_BANKS, :]
                pe.matmul(bank, q, k_pair[:, h, cols], start=True, stop=False)
                pe.matmul(bank, q, k_swap[:, h, cols], start=False, stop=True).then_inc(scores_ready, 1)

            def transposes(j, h, g, early=False):
                if g % 2 == 0:
                    pe.wait_ge(exp_done, PIECES * (2 * j + h) + g // 2 + 1)
                unit = 2 * j + h
                if g >= 2:
                    wait_pt(pe, unit, g - 2)
                elif not (early and h == 0):
                    wait_pt(pe, unit - 1, g + NC - 2)
                for t in range(TPC):
                    ins = pe.transpose(ps[:, TR0 + g % 2, t * P:(t + 1) * P],
                                       prob[:, h, g * CH + t * P:g * CH + (t + 1) * P], ident[:, :])
                ins.then_inc(transposed, 1)

            def attend(j, h, g, first=False):
                wait_pt(pe, 2 * j + h, g)
                if g == 0 and not first:
                    pe.wait_ge(sat_ready, 2 * (j - 1) + h + 1)
                    if h == 1:
                        pe.wait_ge(o_read, j)
                for t in range(TPC):
                    ins = pe.matmul(ps[:, AV0 + h, 0:DV1], prob_t[:, g % PT_RING, t * P:(t + 1) * P],
                                    v_sb[:, g * TPC + t, h, :], start=(g == 0 and t == 0),
                                    stop=(g == NC - 1 and t == TPC - 1))
                ins.then_inc(av_done, 1)

            def sat_transpose(j):
                pe.wait_ge(sat_ready, 2 * j + 2)
                if not isinstance(j, int) or j >= 1:
                    pe.wait_ge(satt_ready, j)
                pe.transpose(ps[:, AV0 + 1, P:2 * P], sat[:, :], ident[:, :]).then_inc(satt_psum, 1)

            def out_project(j):
                pe.wait_ge(satt_ready, j + 1)
                pe.matmul(ps[:, AV0 + 1, 2 * P:3 * P], sat_t[:, :], wrd[:, j // (NT // 2), :],
                          start=True, stop=True).then_inc(o_psum, 1)

            def step(i, par, prior=True, now=True, post=True, early=False):
                for h in range(HEADS):
                    for g in range(NC):
                        if now:
                            scores(i, h, g)
                        if prior:
                            transposes(i - 1, h, g, early)
                            if g >= LAG:
                                attend(i - 1, h, g - LAG, early)
                            elif h == 1:
                                attend(i - 1, 0, g + NC - LAG)
                            elif post:
                                attend(i - 2, 1, g + NC - LAG)
                        if post and h == 0 and g == 5:
                            sat_transpose(i - 2)
                        if post and h == 0 and g == 7:
                            out_project(i - 2)

            step(0, 0, prior=False, post=False)
            step(1, 1, post=False, early=True)
            pairs(pe, 2, NT, step)
            step(NT, 0, now=False)
            for g in range(NC - LAG, NC):
                attend(NT - 1, 1, g)
            sat_transpose(NT - 1)
            out_project(NT - 1)

            pe.wait_ge(ffn_w_in, 48)

            def x2_transpose(j, par):
                pe.wait_ge(x2_ready, j + 1)
                if not isinstance(j, int) or j >= 1:
                    pe.wait_ge(acc_ready, j)
                for t in range(TPC):
                    ins = pe.transpose(ps[:, TR0, t * P:(t + 1) * P], x2[:, par, t, :], ident[:, :])
                ins.then_inc(x2t_psum, 1)

            def logits(j, par):
                pe.wait_ge(x2t_ready, j + 1)
                if not isinstance(j, int) or j >= 1:
                    pe.wait_ge(gatet_ready, j)
                for t in range(TPC):
                    ins = pe.matmul(ps[:, TR0 + 1, t * E:(t + 1) * E], x2_t[:, par, t * P:(t + 1) * P], wg_sb[:, :],
                                    start=True, stop=True)
                ins.then_inc(logit_psum, 1)

            def gate_transpose(j, par):
                pe.wait_ge(gate_ready, j + 1)
                for t in range(TPC):
                    ins = pe.transpose(ps[0:E, TR0 + 1, t * P:(t + 1) * P], gate[:, par, t, :], ident[:, :])
                ins.then_inc(gatet_psum, 1)

            def gates_b2(j):
                pe.wait_ge(gatet_ready, j + 1)
                for t in range(TPC):
                    ins = pe.matmul(ps[:, TR0, t * P:(t + 1) * P], gate_t[:, t * P:(t + 1) * P], b2_sb[:, :],
                                    start=True, stop=True)
                ins.then_inc(b2_psum, 1)

            def up(j, par, e, early=False):
                for b in range(HB):
                    slot = (2 * e + b) % 4
                    if not (early and e < 2):
                        pe.wait_ge(hid_ready, 16 * j + 2 * e + b - 3)
                    pe.matmul(ps[:, slot, :], w1_sb[:, e, b * P:(b + 1) * P], x2_t[:, par, :],
                              start=True, stop=True).then_inc(up_done, 1)

            def down(j, e, early=False):
                pe.wait_ge(hid_ready, 16 * j + 2 * e + 2)
                if not (early and e < 2):
                    pe.wait_ge(combined, 8 * j + e - 1)
                for t in range(TPC):
                    for b in range(HB):
                        ins = pe.matmul(ps[:, AV0 + e % 2, t * D:(t + 1) * D],
                                        hid[:, (2 * e + b) % 4, t * P:(t + 1) * P], w2_sb[:, e, b, :],
                                        start=(b == 0), stop=(b == HB - 1))
                ins.then_inc(down_done, 1)

            def ffn(j, par, prep=True, early=False):
                for e in range(E):
                    up(j, par, e, early)
                    if e >= 1:
                        down(j, e - 1, early)
                    elif not early:
                        down(j - 1, E - 1)
                    if prep and e == 0:
                        x2_transpose(j + 1, 1 - par)
                    if prep and e == 2:
                        logits(j + 1, 1 - par)
                    if prep and e == 5:
                        gate_transpose(j + 1, 1 - par)
                    if prep and e == 6:
                        gates_b2(j + 1)

            x2_transpose(0, 0)
            logits(0, 0)
            gate_transpose(0, 0)
            gates_b2(0)
            ffn(0, 0, early=True)
            ffn(1, 1)
            pairs(pe, 2, NC - 2, ffn)
            ffn(NC - 2, 0)
            ffn(NC - 1, 1, prep=False)
            down(NC - 1, E - 1)


INPUTS = ["x", "adj", "L0_gnn_Wq", "L0_gnn_Wk", "L0_gnn_Wv", "L0_gnn_weightr", "L0_gnn_weightd", "L0_gnn_bias",
          "L0_ffn_Wg", "L0_ffn_bg", "L0_ffn_W1", "L0_ffn_b1", "L0_ffn_W2", "L0_ffn_b2"]


def kernel(**inputs):
    import numpy as np
    import concourse.bacc as bacc
    from concourse.bass_utils import run_bass_kernel_spmd

    nc = bacc.Bacc("TRN2", target_bir_lowering=False, num_devices=1)
    arrays, aps = {}, []
    for name in INPUTS:
        a = np.ascontiguousarray(inputs[name])
        arrays[f"in_{name}"] = a
        aps.append(nc.dram_tensor(f"in_{name}", a.shape, mybir.dt.from_np(a.dtype), kind="ExternalInput").ap())
    aps.append(nc.dram_tensor("out", (N, D), F32, kind="ExternalOutput").ap())
    build(nc, *aps)
    r = run_bass_kernel_spmd(nc, [arrays], core_ids=[0])
    return r.results[0]["out"]
```

```python
from contextlib import ExitStack

import concourse.bass as bass
from concourse import mybir

F32 = mybir.dt.float32
F16 = mybir.dt.float16
BF16 = mybir.dt.bfloat16
I32 = mybir.dt.int32
ALU = mybir.AluOpType
ACT = mybir.ActivationFunctionType
AX_X = mybir.AxisListType.X

P = 128
N, D = 4096, 128
HEADS = 2
DH = D // HEADS
SCALE = float(DH) ** -0.5
EPS = 1e-5
SLOPE = 0.01
BIG = 2.0 ** 64
NT = N // P
CH = 512
NC = N // CH
TPC = CH // P
E, H, HB = 8, 256, 2
HALF = N // 2
W_UP = 2.0 ** 8
PIECES = 4
PIECE = N // PIECES

SCORE_BANKS = 2
TR0, TR_BANKS, AV0 = 2, 4, 6
PREP0 = 4
VW = 2 * DH + 2
PT_RING = 4
LAG = 3
POOL_GROUPS = (1, 4, 6)
DVE_GROUPS = tuple(g for g in range(NC) if g not in POOL_GROUPS)


def build(nc, x, adj, wq, wk, wv, wr, wd, bias, wg, bg, w1, b1, w2, b2, out):
    with ExitStack() as ctx:
        def sb(name, shape, dt):
            return ctx.enter_context(nc.sbuf_tensor(name, shape, dt))

        def sem(name):
            return ctx.enter_context(nc.semaphore(name))

        ident = sb("ident", [P, P], F32)
        x_sb = sb("x_sb", [P, NT, D], F32)
        mask = sb("mask", [P, 2, N], BF16)
        prob = sb("prob", [P, HEADS, N], F32)
        pt_hi = sb("pt_hi", [P, PT_RING, CH], F16)
        pt_lo = sb("pt_lo", [P, PT_RING, CH], F16)
        pt_raw = sb("pt_raw", [P, len(POOL_GROUPS), CH], F32)
        q_pair = sb("q_pair", [P, HEADS, N], F16)
        k_pair = sb("k_pair", [P, HEADS, N], F16)
        k_swap = sb("k_swap", [P, HEADS, N], F16)
        v_pair = sb("v_pair", [P, NT, HEADS, VW], F16)
        sat = sb("sat", [P, NT, D], F32)
        wq2 = sb("wq2", [P, HEADS, 2, DH], F32)
        wk2 = sb("wk2", [P, HEADS, 2, DH], F32)
        wv_sb = sb("wv_sb", [P, D], F32)
        wrd = sb("wrd", [P, 2, D], F32)
        bias_b = sb("bias_b", [P, D], F32)
        wg_sb = sb("wg_sb", [P, E], F32)
        bg_b = sb("bg_b", [P, E], F32)
        b1_sb = sb("b1_sb", [P, E, HB], F32)
        b2_sb = sb("b2_sb", [E, D], F32)
        w1_pair = sb("w1_pair", [P, 2, E * H], F16)
        w2_pair = sb("w2_pair", [P, 2, E * HB * D], F16)
        stats = sb("stats", [P, 8, 6], F32)
        mv = sb("mv", [P, NT, 2], F32)
        ve = sb("ve", [P, NT], F32)
        rstd = sb("rstd", [P, NT], F32)
        expo = sb("expo", [P, NT], F32)
        low = sb("low", [P, HEADS, NC], F32)
        nmax = sb("nmax", [P, HEADS], F32)
        rsum = sb("rsum", [P, HEADS], F32)
        av_lo = sb("av_lo", [P, DH], F32)

        def area(h, first, n):
            return prob[:, h, first * CH:(first + n) * CH]

        xn = area(0, 0, 2).rearrange("p (r t d) -> p r t d", r=2, t=TPC)
        xn_t = area(0, 2, 2).rearrange("p (r c) -> p r c", r=2)
        w1_raw = area(0, 4, 4)
        w2_raw = area(1, 4, 4)
        sat_st = area(0, 0, 1).rearrange("p (t d) -> p t d", t=TPC)
        sat_t = area(0, 1, 1)
        o_pre = area(0, 2, 1).rearrange("p (t d) -> p t d", t=TPC)
        o_act = area(0, 3, 1).rearrange("p (t d) -> p t d", t=TPC)
        x2 = area(0, 4, 1).rearrange("p (t d) -> p t d", t=TPC)
        x2_t = area(0, 5, 1)
        x2t_hi = area(0, 6, 1).bitcast(F16).rearrange("p (r c) -> p r c", r=2)
        x2t_lo = area(0, 7, 1).bitcast(F16).rearrange("p (r c) -> p r c", r=2)
        acc = area(1, 0, 2).rearrange("p (r t d) -> p r t d", r=2, t=TPC)
        hid = area(1, 2, 4).rearrange("p (r c) -> p r c", r=4)
        gate_t = prob[0:E, 1, 6 * CH:7 * CH]
        small = area(1, 7, 1)
        fields = [small[:, 32 * k:32 * (k + 1)].rearrange("p (t e) -> p t e", e=E) for k in range(8)]
        logit, top8, above, tied, rank, keep, gate0, gate1 = fields
        gate = [gate0, gate1]
        chosen = small[:, 256:288].rearrange("p (t e) -> p t e", e=E)
        mv2 = small[:, 288:296].rearrange("p (t s) -> p t s", s=2)
        ve2, rstd2 = small[:, 296:300], small[:, 300:304]
        hid_hi, hid_lo = pt_hi, pt_lo

        ps = ctx.enter_context(nc.psum_tensor("ps", [P, 8, CH], F32))

        x_in = [sem(f"x_in{i}") for i in range(4)]
        w_in = sem("w_in")
        ffn_w_in = sem("ffn_w_in")
        b1_in = sem("b1_in")
        w_split_chain = sem("w_split_chain")
        adj_in = [sem(f"adj_in{q}") for q in range(2)]
        swap_in = sem("swap_in")
        out_done = [sem(f"out_done{r}") for r in range(2)]
        ident_zero = sem("ident_zero")
        ident_ready = sem("ident_ready")
        ones_ready = sem("ones_ready")
        mask_ready = sem("mask_ready")
        stats_chain = sem("stats_chain")
        var_ready = sem("var_ready")
        rstd_ready = sem("rstd_ready")
        xn_ready = sem("xn_ready")
        xnt_psum = sem("xnt_psum")
        xnt_ready = sem("xnt_ready")
        proj_psum = sem("proj_psum")
        hi_ready = sem("hi_ready")
        lo_ready = sem("lo_ready")
        v_psum = sem("v_psum")
        v_hi_ready = sem("v_hi_ready")
        v_lo_ready = sem("v_lo_ready")
        scores_ready = sem("scores_ready")
        masked = sem("masked")
        max_ready = sem("max_ready")
        exp_done = sem("exp_done")
        transposed = sem("transposed")
        pt_hi_ready = sem("pt_hi_ready")
        pt_raw_ready = sem("pt_raw_ready")
        pt_pool_hi = sem("pt_pool_hi")
        pt_by_dve = sem("pt_by_dve")
        pt_by_pool = sem("pt_by_pool")
        av_done = sem("av_done")
        sum_inv = sem("sum_inv")
        av_lo_ready = sem("av_lo_ready")
        sat_ready = sem("sat_ready")
        sat_staged = sem("sat_staged")
        satt_psum = sem("satt_psum")
        satt_ready = sem("satt_ready")
        o_psum = sem("o_psum")
        post_chain = sem("post_chain")
        ve2_ready = sem("ve2_ready")
        rstd2_ready = sem("rstd2_ready")
        x2_ready = sem("x2_ready")
        x2t_psum = sem("x2t_psum")
        x2t_ready = sem("x2t_ready")
        x2t_lo_ready = sem("x2t_lo_ready")
        logit_psum = sem("logit_psum")
        gate_chain = sem("gate_chain")
        gate_ready = sem("gate_ready")
        b2_scaled = sem("b2_scaled")
        gatet_psum = sem("gatet_psum")
        gatet_ready = sem("gatet_ready")
        b2_psum = sem("b2_psum")
        acc_ready = sem("acc_ready")
        up_done = sem("up_done")
        hid_raw_ready = sem("hid_raw_ready")
        hid_hi_ready = sem("hid_hi_ready")
        hid_lo_ready = sem("hid_lo_ready")
        down_done = sem("down_done")
        combined = sem("combined")

        def pairs(eng, first, end, body):
            with eng.Fori(0, (end - first) // 2) as k:
                body(2 * k + first, first % 2)
                body(2 * k + first + 1, (first + 1) % 2)

        def wait_tr_read(eng, unit, g):
            if g in POOL_GROUPS:
                eng.wait_ge(pt_raw_ready, len(POOL_GROUPS) * unit + POOL_GROUPS.index(g) + 1)
            else:
                eng.wait_ge(pt_by_dve, len(DVE_GROUPS) * unit + DVE_GROUPS.index(g) + 1)

        def wait_pt(eng, unit, g):
            if g in POOL_GROUPS:
                eng.wait_ge(pt_by_pool, len(POOL_GROUPS) * unit + POOL_GROUPS.index(g) + 1)
            else:
                eng.wait_ge(pt_by_dve, len(DVE_GROUPS) * unit + DVE_GROUPS.index(g) + 1)

        block = ctx.enter_context(nc.Block())
        N_W = 11
        X_PARTS, X_TILES = 4, NT // 4

        @block.sync
        def _(sp):
            xv = x.rearrange("(t p) d -> p t d", p=P)
            for i in range(X_PARTS):
                part = slice(i * X_TILES, (i + 1) * X_TILES)
                sp.dma_start(x_sb[:, part, :], xv[:, part, :]).then_inc(x_in[i], 16)

            sp.dma_start(w1_raw.rearrange("p (e h) -> p e h", e=E), w1.rearrange("e d h -> d e h")).then_inc(ffn_w_in, 16)
            sp.dma_start(w2_raw.rearrange("p (e b d) -> p e b d", e=E, b=HB),
                         w2.rearrange("e (b p) d -> p e b d", b=HB)).then_inc(ffn_w_in, 16)
            for c in range(2):
                sp.wait_ge(lo_ready, 4 * (c + 1) * (NC // 2))
                sp.wait_ge(hi_ready, 4 * (c + 1) * (NC // 2))
                cols = slice(c * HALF, (c + 1) * HALF)
                for h in range(HEADS):
                    sp.dma_start(k_swap[0:DH, h, cols], k_pair[DH:P, h, cols]).then_inc(swap_in, 16)
                    sp.dma_start(k_swap[DH:P, h, cols], k_pair[0:DH, h, cols]).then_inc(swap_in, 16)
            ov = out.rearrange("(t p) d -> p t d", p=P)

            def store(j, par):
                sp.wait_ge(combined, E * j + E)
                sp.dma_start(ov[:, bass.ds(j * TPC, TPC), :], acc[:, par]).then_inc(out_done[par], 16)

            pairs(sp, 0, NC, store)
            for r in range(2):
                sp.wait_ge(out_done[r], 16 * NC // 2)

        @block.gpsimd
        def _(pool):
            pool.memset(ident[:, :], 0.0).then_inc(ident_zero, 1)
            pool.wait_ge(ident_zero, 1)
            pool.affine_select(out=ident[:, :], in_=ident[:, :], compare_op=ALU.not_equal, fill=1.0, base=0,
                               pattern=[[-1, P]], channel_multiplier=1).then_inc(ident_ready, 1)
            pool.memset(v_pair[:, :, :, DH:DH + 1], 1.0).then_inc(ones_ready, 1)

            pool.memset(expo[:, :], -0.5).then_inc(ones_ready, 1)

            def load_adj(i, par):
                if not isinstance(i, int) or i >= 2:
                    pool.wait_ge(masked, 16 * (i - 2) + 16)
                pool.dma_start(mask[:, par, :], adj[bass.ds(i * P, P), :], max_dma_last_dim=8192).then_inc(adj_in[par], 16)

            pool.wait_ge(ones_ready, 2)
            for i in range(X_PARTS):
                part = slice(i * X_TILES, (i + 1) * X_TILES)
                pool.wait_ge(var_ready, i + 1)
                pool.tensor_tensor(rstd[:, part], ve[:, part], expo[:, part], ALU.pow).then_inc(rstd_ready, 1)

            load_adj(0, 0)
            load_adj(1, 1)

            pool.wait_ge(ffn_w_in, 32)
            for n, (raw, pair) in enumerate(((w1_raw, w1_pair), (w2_raw, w2_pair))):
                pool.tensor_scalar(raw, raw, W_UP, 0.0, ALU.mult, ALU.add).then_inc(w_split_chain, 1)
                pool.wait_ge(w_split_chain, 3 * n + 1)
                pool.tensor_scalar(pair[:, 0, :], raw, 1.0, 0.0, ALU.mult, ALU.add).then_inc(w_split_chain, 1)
                pool.wait_ge(w_split_chain, 3 * n + 2)
                pool.tensor_tensor(pair[:, 1, :], raw, pair[:, 0, :], ALU.subtract).then_inc(w_split_chain, 1)

            def split_pt(j, h, k):
                g = POOL_GROUPS[k]
                count = len(POOL_GROUPS) * (2 * j + h) + k + 1
                pool.wait_ge(pt_raw_ready, count)
                pool.nop(nofuse=True)
                pool.tensor_scalar(pt_hi[:, g % PT_RING, :], pt_raw[:, k, :], 1.0, 0.0, ALU.mult,
                                   ALU.add).then_inc(pt_pool_hi, 1)
                pool.wait_ge(pt_pool_hi, count)
                pool.tensor_tensor(pt_lo[:, g % PT_RING, :], pt_raw[:, k, :], pt_hi[:, g % PT_RING, :],
                                   ALU.subtract).then_inc(pt_by_pool, 1)

            def step(i, par, ahead=True):
                if ahead:
                    load_adj(i + 1, 1 - par)
                for h in range(HEADS):
                    for k in range(len(POOL_GROUPS)):
                        split_pt(i - 1, h, k)

            step(1, 1)
            pairs(pool, 2, NT - 2, step)
            step(NT - 2, 0)
            step(NT - 1, 1, ahead=False)
            step(NT, 0, ahead=False)

            def inverse_std(j):
                pool.wait_ge(ve2_ready, j + 1)
                pool.tensor_tensor(rstd2, ve2, expo[:, 0:TPC], ALU.pow).then_inc(rstd2_ready, 1)

            def ffn(j, par, prep=True):
                for e in range(E):
                    for b in range(HB):
                        slot = (2 * e + b) % 4
                        pool.wait_ge(hid_hi_ready, 16 * j + 2 * e + b + 1)
                        pool.tensor_tensor(hid_lo[:, slot, :], hid[:, slot, :], hid_hi[:, slot, :],
                                           ALU.subtract).then_inc(hid_lo_ready, 1)
                    if prep and e == 4:
                        inverse_std(j + 1)

            inverse_std(0)
            pairs(pool, 0, NC - 2, ffn)
            ffn(NC - 2, 0)
            ffn(NC - 1, 1, prep=False)

        @block.scalar
        def _(act):
            act.dma_start(wq2[:, :, 0, :], wq.rearrange("d (h c) -> d h c", h=HEADS)).then_inc(w_in, 16)
            act.dma_start(wq2[:, :, 1, :], wq.rearrange("d (h c) -> d h c", h=HEADS)).then_inc(w_in, 16)
            act.dma_start(wk2[:, :, 0, :], wk.rearrange("d (h c) -> d h c", h=HEADS)).then_inc(w_in, 16)
            act.dma_start(wk2[:, :, 1, :], wk.rearrange("d (h c) -> d h c", h=HEADS)).then_inc(w_in, 16)
            act.dma_start(wv_sb[:, :], wv).then_inc(w_in, 16)
            act.dma_start(wrd[:, 0, :], wr).then_inc(w_in, 16)
            act.dma_start(wrd[:, 1, :], wd).then_inc(w_in, 16)
            act.dma_start(bias_b[:, :], bias.rearrange("(a d) -> a d", a=1).to_broadcast([P, D])).then_inc(w_in, 16)
            act.dma_start(wg_sb[:, :], wg).then_inc(w_in, 16)
            act.dma_start(bg_b[:, :], bg.rearrange("(a d) -> a d", a=1).to_broadcast([P, E])).then_inc(w_in, 16)
            act.dma_start(b2_sb[:, :], b2).then_inc(w_in, 16)
            with nc.allow_non_contiguous_dma(reason="2048 values, once"):
                act.dma_start(b1_sb[:, :, :], b1.rearrange("e (b p) -> p e b", p=P)).then_inc(b1_in, 16)

            def copy_xnt(j, par):
                act.wait_ge(xnt_psum, j + 1)
                act.activation(xn_t[:, par, :], ps[:, PREP0 + par, :], ACT.Copy).then_inc(xnt_ready, 1)

            def project(j, par, ahead=True):
                cols = bass.ds(j * CH, CH)
                for m, (dst, scale) in enumerate(((q_pair, SCALE), (k_pair, 1.0))):
                    for h in range(HEADS):
                        act.wait_ge(proj_psum, 4 * j + 2 * m + h + 1)
                        act.activation(dst[:, h, cols], ps[:, 2 * m + h, :], ACT.Copy, scale=scale).then_inc(hi_ready, 1)
                act.wait_ge(v_psum, j + 1)
                act.activation(v_pair[:, bass.ds(j * TPC, TPC), :, 0:DH],
                               ps[:, AV0 + par, :].rearrange("p (t h c) -> p t h c", t=TPC, h=HEADS),
                               ACT.Copy).then_inc(v_hi_ready, 1)
                if ahead:
                    copy_xnt(j + 2, par)

            copy_xnt(0, 0)
            copy_xnt(1, 1)
            project(0, 0)
            project(1, 1)
            pairs(act, 2, NC - 2, project)
            project(NC - 2, 0, ahead=False)
            project(NC - 1, 1, ahead=False)

            act.wait_ge(w_split_chain, 6)

            def exp_piece(j, h, n):
                if n == 0:
                    act.wait_ge(max_ready, 2 * j + h + 1)
                cols = slice(n * PIECE, (n + 1) * PIECE)
                act.activation(prob[:, h, cols], prob[:, h, cols], ACT.Exp, bias=nmax[:, h:h + 1],
                               scale=-1.0).then_inc(exp_done, 1)

            def split_pt(j, h, g, early=False):
                act.wait_ge(transposed, 16 * j + 8 * h + g + 1)
                if not (early and h == 0 and g < PT_RING):
                    act.wait_ge(av_done, 16 * j + 8 * h + g - PT_RING + 1)
                if g in POOL_GROUPS:
                    act.activation(pt_raw[:, POOL_GROUPS.index(g), :], ps[:, TR0 + g % TR_BANKS, :],
                                   ACT.Copy).then_inc(pt_raw_ready, 1)
                else:
                    act.activation(pt_hi[:, g % PT_RING, :], ps[:, TR0 + g % TR_BANKS, :],
                                   ACT.Copy).then_inc(pt_hi_ready, 1)

            def step(i, prior=True, now=True, early=False):
                for h in range(HEADS):
                    has_exp = prior if h == 0 else now
                    ej, eh = (i - 1, 1) if h == 0 else (i, 0)
                    for g in range(NC):
                        if prior:
                            split_pt(i - 1, h, g, early)
                        if has_exp and g % 2 == 1:
                            exp_piece(ej, eh, g // 2)

            step(0, prior=False)
            step(1, early=True)
            pairs(act, 2, NT, lambda i, par: step(i))
            step(NT, now=False)

            act.wait_ge(b1_in, 16)

            def satt_copy(j):
                act.wait_ge(satt_psum, j + 1)
                act.activation(sat_t, ps[:, PREP0 + 1, :], ACT.Copy).then_inc(satt_ready, 1)

            def x2t_copy(j, par):
                act.wait_ge(x2t_psum, j + 1)
                act.activation(x2t_hi[:, par, :], ps[:, PREP0 + 1, :], ACT.Copy).then_inc(x2t_ready, 1)
                act.activation(x2_t, ps[:, PREP0 + 1, :], ACT.Copy).then_inc(x2t_ready, 1)

            def gatet_copy(j):
                act.wait_ge(gatet_psum, j + 1)
                act.activation(gate_t, ps[0:E, PREP0, :], ACT.Copy).then_inc(gatet_ready, 1)

            def ffn(j, par, prep=True, early=False):
                for e in range(E):
                    for b in range(HB):
                        slot = (2 * e + b) % 4
                        act.wait_ge(up_done, 16 * j + 2 * e + b + 1)
                        if not (early and e < 2):
                            act.wait_ge(down_done, 8 * j + e - 1)
                        act.activation(hid[:, slot, :], ps[:, slot, :], ACT.Gelu, bias=b1_sb[:, e, b:b + 1],
                                       scale=1.0 / W_UP).then_inc(hid_raw_ready, 1)
                        act.wait_ge(hid_raw_ready, 16 * j + 2 * e + b + 1)
                        act.activation(hid_hi[:, slot, :], hid[:, slot, :], ACT.Copy).then_inc(hid_hi_ready, 1)
                    if prep and e == 1:
                        satt_copy(j + 1)
                    if e == 2:
                        gatet_copy(j)
                    if prep and e == 6:
                        x2t_copy(j + 1, 1 - par)

            satt_copy(0)
            x2t_copy(0, 0)
            ffn(0, 0, early=True)
            ffn(1, 1)
            pairs(act, 2, NC - 2, ffn)
            ffn(NC - 2, 0)
            ffn(NC - 1, 1, prep=False)

        @block.vector
        def _(dve):
            def linker(s, base):
                count = [base]

                def link(ins):
                    count[0] = count[0] + 1
                    ins.then_inc(s, 1)
                    dve.wait_ge(s, count[0])
                return link

            def settled():
                dve.nop(nofuse=True)

            def row_statistics(i):
                dve.wait_ge(x_in[i], 16)
                for t in range(X_TILES):
                    ins = dve.bn_stats(stats[:, t, :], x_sb[:, X_TILES * i + t, :])
                ins.then_inc(stats_chain, 1)
                dve.wait_ge(stats_chain, 2 * i + 1)
                for t in range(X_TILES):
                    ins = dve.bn_aggr(mv[:, X_TILES * i + t, :], stats[:, t, :])
                ins.then_inc(stats_chain, 1)
                dve.wait_ge(stats_chain, 2 * i + 2)
                part = slice(i * X_TILES, (i + 1) * X_TILES)
                dve.tensor_scalar(ve[:, part], mv[:, part, 1], EPS, None, ALU.add).then_inc(var_ready, 1)

            def normalise_x(j, par):
                for t in range(TPC):
                    tile = j * TPC + t
                    ins = dve.tensor_scalar(xn[:, par, t, :], x_sb[:, tile, :], mv[:, tile, 0:1],
                                            rstd[:, bass.ds(tile, 1)], ALU.subtract, ALU.mult)
                ins.then_inc(xn_ready, 1)

            def project(j, par, ahead=True):
                if ahead:
                    dve.wait_ge(xnt_psum, j + 1)
                    normalise_x(j + 2, par)
                cols = bass.ds(j * CH, CH)
                for m, (pair, scale) in enumerate(((q_pair, SCALE), (k_pair, 1.0))):
                    for h in range(HEADS):
                        dve.wait_ge(hi_ready, 4 * j + 2 * m + h + 1)
                        lo = pair[DH:P, h, cols]
                        dve.scalar_tensor_tensor(lo, ps[DH:P, 2 * m + h, :], scale, lo, ALU.mult,
                                                 ALU.subtract).then_inc(lo_ready, 1)
                dve.wait_ge(v_hi_ready, j + 1)
                tiles = bass.ds(j * TPC, TPC)
                dve.tensor_tensor(v_pair[:, tiles, :, DH + 1:2 * DH + 1],
                                  ps[:, AV0 + par, :].rearrange("p (t h c) -> p t h c", t=TPC, h=HEADS),
                                  v_pair[:, tiles, :, 0:DH], ALU.subtract).then_inc(v_lo_ready, 1)

            row_statistics(0)
            row_statistics(1)
            dve.wait_ge(rstd_ready, 1)
            normalise_x(0, 0)
            normalise_x(1, 1)
            row_statistics(2)
            row_statistics(3)
            dve.wait_ge(rstd_ready, X_PARTS)
            project(0, 0)
            project(1, 1)
            pairs(dve, 2, NC - 2, project)
            project(NC - 2, 0, ahead=False)
            project(NC - 1, 1, ahead=False)

            def make_mask(i, par, half):
                dve.wait_ge(adj_in[par], 8 * i - 8 * par + 16)
                part = mask[:, par, half * HALF:(half + 1) * HALF]
                dve.tensor_scalar(part, part, 0.0, -BIG, ALU.is_le, ALU.mult).then_inc(mask_ready, 1)

            def mask_scores(i, par, h, c):
                if c == 0:
                    dve.wait_ge(mask_ready, 2 * i + 2)
                dve.wait_ge(scores_ready, 16 * i + 8 * h + c + 1)
                cols = slice(c * CH, (c + 1) * CH)
                settled()
                dve.tensor_tensor_reduce(out=prob[:, h, cols], in0=ps[:, c % SCORE_BANKS, :], in1=mask[:, par, cols],
                                         scale=-1.0, scalar=3.0e38, op0=ALU.add, op1=ALU.min,
                                         accum_out=low[:, h, c:c + 1]).then_inc(masked, 1)

            def split_pt(j, h, g):
                dve.wait_ge(pt_hi_ready, len(DVE_GROUPS) * (2 * j + h) + DVE_GROUPS.index(g) + 1)
                dve.tensor_tensor(pt_lo[:, g % PT_RING, :], ps[:, TR0 + g % TR_BANKS, :], pt_hi[:, g % PT_RING, :],
                                  ALU.subtract).then_inc(pt_by_dve, 1)

            def finish_head(j, h):
                acc_h = ps[:, AV0 + h, :]
                dve.wait_ge(av_done, 16 * j + 8 * h + 8)
                dve.reciprocal(rsum[:, h:h + 1], acc_h[:, DH:DH + 1]).then_inc(sum_inv, 1)
                dve.wait_ge(sum_inv, 2 * j + h + 1)
                dve.tensor_scalar(av_lo[:, :], acc_h[:, DH + 1:2 * DH + 1], rsum[:, h:h + 1], None,
                                  ALU.mult).then_inc(av_lo_ready, 1)
                dve.wait_ge(av_lo_ready, 2 * j + h + 1)
                dve.scalar_tensor_tensor(sat[:, j, h * DH:(h + 1) * DH], acc_h[:, 0:DH], rsum[:, h:h + 1], av_lo[:, :],
                                         ALU.mult, ALU.add).then_inc(sat_ready, 1)

            def step(i, par, prior=True, now=True, post=True, ahead=True):
                for h in range(HEADS):
                    for c in range(NC):
                        if now:
                            mask_scores(i, par, h, c)
                        if prior and c in DVE_GROUPS:
                            split_pt(i - 1, h, c)
                        if c == 4 and h == 0 and post:
                            finish_head(i - 2, 1)
                        if c == 4 and h == 1 and prior:
                            finish_head(i - 1, 0)
                        if ahead and h == 1 and c in (1, 6):
                            make_mask(i + 1, 1 - par, c // 6)
                    if now:
                        dve.wait_ge(masked, 16 * i + 8 * h + 8)
                        dve.tensor_reduce(nmax[:, h:h + 1], low[:, h, :], AX_X, ALU.min).then_inc(max_ready, 1)

            make_mask(0, 0, 0)
            make_mask(0, 0, 1)
            dve.wait_ge(w_split_chain, 6)
            step(0, 0, prior=False, post=False)
            step(1, 1, post=False)
            pairs(dve, 2, NT - 2, step)
            step(NT - 2, 0)
            step(NT - 1, 1, ahead=False)
            step(NT, 0, now=False, ahead=False)
            finish_head(NT - 1, 1)

            dve.wait_ge(sat_ready, 2 * NT)
            dve.tensor_scalar(b2_sb[:, :], b2_sb[:, :], W_UP, None, ALU.mult).then_inc(b2_scaled, 1)

            def stage_sat(j):
                if not isinstance(j, int) or j >= 1:
                    dve.wait_ge(satt_psum, j)
                dve.tensor_copy(sat_st, sat[:, bass.ds(j * TPC, TPC), :]).then_inc(sat_staged, 1)

            POST = 3

            def residual(j, par):
                link = linker(post_chain, POST * j)
                dve.wait_ge(o_psum, j + 1)
                link(dve.tensor_tensor(o_pre, ps[:, PREP0 + 1, :].rearrange("p (t d) -> p t d", d=D),
                                       bias_b[:, :].unsqueeze(1).to_broadcast([P, TPC, D]), ALU.add))
                link(dve.scalar_tensor_tensor(o_act, o_pre, SLOPE, o_pre, ALU.mult, ALU.max))
                if not isinstance(j, int) or j >= 2:
                    dve.wait_ge(out_done[par], 8 * j - 8 * par)
                link(dve.tensor_tensor(acc[:, par], x_sb[:, bass.ds(j * TPC, TPC), :], o_act, ALU.add))

            def statistics(j, par):
                settled()
                for t in range(TPC):
                    ins = dve.bn_stats(stats[:, t, :], acc[:, par, t, :])
                ins.then_inc(stats_chain, 1)
                dve.wait_ge(stats_chain, 2 * j + 9)
                settled()
                for t in range(TPC):
                    ins = dve.bn_aggr(mv2[:, t, :], stats[:, t, :])
                ins.then_inc(stats_chain, 1)
                dve.wait_ge(stats_chain, 2 * j + 10)
                dve.tensor_scalar(ve2, mv2[:, :, 1], EPS, None, ALU.add).then_inc(ve2_ready, 1)

            def normalise(j, par):
                dve.wait_ge(rstd2_ready, j + 1)
                for t in range(TPC):
                    ins = dve.tensor_scalar(x2[:, t, :], acc[:, par, t, :], mv2[:, t, 0:1], rstd2[:, t:t + 1],
                                            ALU.subtract, ALU.mult)
                ins.then_inc(x2_ready, 1)

            def x2t_low(j, par):
                dve.wait_ge(x2t_ready, 2 * j + 2)
                dve.tensor_tensor(x2t_lo[:, par, :], ps[:, PREP0 + 1, :], x2t_hi[:, par, :],
                                  ALU.subtract).then_inc(x2t_lo_ready, 1)

            STEPS = 14

            def rank_gates(j):
                link = linker(gate_chain, STEPS * j)
                dve.wait_ge(logit_psum, j + 1)
                link(dve.tensor_tensor(logit, ps[:, PREP0, 0:TPC * E].rearrange("p (t e) -> p t e", e=E),
                                       bg_b[:, :].unsqueeze(1).to_broadcast([P, TPC, E]), ALU.add))
                settled()
                for t in range(TPC):
                    ins = dve.max(top8[:, t, :], logit[:, t, :])
                link(ins)
                second = top8[:, :, 1:2].to_broadcast([P, TPC, E])
                dve.tensor_tensor(above, logit, second, ALU.is_gt)
                link(dve.tensor_tensor(tied, logit, second, ALU.is_equal))
                link(dve.tensor_reduce(rank[:, :, 0:1], above, AX_X, ALU.add))
                for e in range(1, E):
                    link(dve.tensor_tensor(rank[:, :, e:e + 1], rank[:, :, e - 1:e], tied[:, :, e - 1:e], ALU.add))

            def choose_gates(j, par):
                link = linker(gate_chain, STEPS * j + 11)
                link(dve.scalar_tensor_tensor(keep, rank, 2.0, tied, ALU.is_lt, ALU.mult))
                link(dve.tensor_tensor(chosen, keep, above, ALU.add))
                link(dve.tensor_scalar(gate[par], chosen, 1.0 / W_UP, None, ALU.mult))

            def add_b2(j, par):
                dve.wait_ge(b2_psum, j + 1)
                dve.wait_ge(combined, 8 * j + 3)
                dve.tensor_tensor(acc[:, par], ps[:, PREP0, :].rearrange("p (t d) -> p t d", d=D), acc[:, par],
                                  ALU.add).then_inc(acc_ready, 1)

            def combine(j, par, e):
                dve.wait_ge(down_done, 8 * j + e + 1)
                if e == 0:
                    dve.wait_ge(gate_chain, 14 * j + 14)
                elif e == 3:
                    dve.wait_ge(acc_ready, j + 1)
                else:
                    dve.wait_ge(combined, 8 * j + e)
                for t in range(TPC):
                    ins = dve.scalar_tensor_tensor(acc[:, par, t, :], ps[:, AV0 + e % 2, t * D:(t + 1) * D],
                                                   gate[par][:, t, e:e + 1], acc[:, par, t, :], ALU.mult, ALU.add)
                ins.then_inc(combined, 1)

            def ffn(j, par, prep=True, stage=True):
                for e in range(E):
                    combine(j, par, e)
                    if prep and e == 1:
                        residual(j + 1, 1 - par)
                    if e == 2:
                        add_b2(j, par)
                        if prep:
                            statistics(j + 1, 1 - par)
                    if prep and e == 3:
                        normalise(j + 1, 1 - par)
                    if stage and e == 4:
                        stage_sat(j + 2)
                    if prep and e == 5:
                        x2t_low(j + 1, 1 - par)
                    if prep and e == 6:
                        rank_gates(j + 1)
                    if prep and e == 7:
                        choose_gates(j + 1, 1 - par)

            stage_sat(0)
            residual(0, 0)
            stage_sat(1)
            statistics(0, 0)
            normalise(0, 0)
            x2t_low(0, 0)
            rank_gates(0)
            choose_gates(0, 0)
            ffn(0, 0)
            ffn(1, 1)
            pairs(dve, 2, NC - 2, ffn)
            ffn(NC - 2, 0, stage=False)
            ffn(NC - 1, 1, prep=False, stage=False)

        @block.tensor
        def _(pe):
            def transpose_x(j, par):
                pe.wait_ge(xn_ready, j + 1)
                for t in range(TPC):
                    ins = pe.transpose(ps[:, PREP0 + par, t * P:(t + 1) * P], xn[:, par, t, :], ident[:, :])
                ins.then_inc(xnt_psum, 1)

            def project(j, par, ahead=True):
                pe.wait_ge(xnt_ready, j + 1)
                for m, w in enumerate((wq2, wk2)):
                    for h in range(HEADS):
                        if not isinstance(j, int) or j > 0:
                            pe.wait_ge(lo_ready, 4 * (j - 1) + 2 * m + h + 1)
                        pe.matmul(ps[:, 2 * m + h, :], w[:, h, :, :].rearrange("d r c -> d (r c)"), xn_t[:, par, :],
                                  start=True, stop=True).then_inc(proj_psum, 1)
                if ahead:
                    transpose_x(j + 2, par)
                if not isinstance(j, int) or j >= 2:
                    pe.wait_ge(v_lo_ready, j - 1)
                for t in range(TPC):
                    ins = pe.matmul(ps[:, AV0 + par, t * P:(t + 1) * P], xn_t[:, par, t * P:(t + 1) * P], wv_sb[:, :],
                                    start=True, stop=True)
                ins.then_inc(v_psum, 1)

            pe.wait_ge(ident_ready, 1)
            transpose_x(0, 0)
            transpose_x(1, 1)
            pe.wait_ge(w_in, 16 * N_W)
            project(0, 0)
            project(1, 1)
            pairs(pe, 2, NC - 2, project)
            project(NC - 2, 0, ahead=False)
            project(NC - 1, 1, ahead=False)
            pe.wait_ge(lo_ready, 4 * NC)
            pe.wait_ge(v_lo_ready, NC)
            pe.wait_ge(ones_ready, 2)
            pe.wait_ge(swap_in, 16 * 8)

            def scores(i, h, c):
                if not (isinstance(i, int) and i == 0 and h == 0 and c < SCORE_BANKS):
                    pe.wait_ge(masked, 16 * i + 8 * h + c - SCORE_BANKS + 1)
                q = q_pair[:, h, bass.ds(i * P, P)]
                cols = slice(c * CH, (c + 1) * CH)
                bank = ps[:, c % SCORE_BANKS, :]
                pe.matmul(bank, q, k_pair[:, h, cols], start=True, stop=False)
                pe.matmul(bank, q, k_swap[:, h, cols], start=False, stop=True).then_inc(scores_ready, 1)

            def transposes(j, h, g, early=False):
                if g % 2 == 0:
                    pe.wait_ge(exp_done, PIECES * (2 * j + h) + g // 2 + 1)
                unit = 2 * j + h
                if g >= TR_BANKS:
                    wait_tr_read(pe, unit, g - TR_BANKS)
                elif not (early and h == 0):
                    wait_tr_read(pe, unit - 1, g + NC - TR_BANKS)
                for t in range(TPC):
                    ins = pe.transpose(ps[:, TR0 + g % TR_BANKS, t * P:(t + 1) * P],
                                       prob[:, h, g * CH + t * P:g * CH + (t + 1) * P], ident[:, :])
                ins.then_inc(transposed, 1)

            def attend(j, h, g, first=False):
                wait_pt(pe, 2 * j + h, g)
                if g == 0 and not first:
                    pe.wait_ge(sat_ready, 2 * (j - 1) + h + 1)
                for t in range(TPC):
                    tile = g * TPC + t
                    pe.matmul(ps[:, AV0 + h, 0:2 * DH + 1], pt_hi[:, g % PT_RING, t * P:(t + 1) * P],
                              v_pair[:, tile, h, 0:2 * DH + 1], start=(tile == 0), stop=False)
                    ins = pe.matmul(ps[:, AV0 + h, 0:DH + 1], pt_lo[:, g % PT_RING, t * P:(t + 1) * P],
                                    v_pair[:, tile, h, 0:DH + 1], start=False, stop=(tile == NT - 1))
                ins.then_inc(av_done, 1)

            def step(i, par, prior=True, now=True, post=True, early=False):
                for h in range(HEADS):
                    for g in range(NC):
                        if prior:
                            transposes(i - 1, h, g, early)
                        if now:
                            scores(i, h, g)
                        if prior:
                            if g >= LAG:
                                attend(i - 1, h, g - LAG, early)
                            elif h == 1:
                                attend(i - 1, 0, g + NC - LAG)
                            elif post:
                                attend(i - 2, 1, g + NC - LAG)

            step(0, 0, prior=False, post=False)
            step(1, 1, post=False, early=True)
            pairs(pe, 2, NT, step)
            step(NT, 0, now=False)
            for g in range(NC - LAG, NC):
                attend(NT - 1, 1, g)

            BANK_A, BANK_B = PREP0, PREP0 + 1

            def sat_transpose(j):
                pe.wait_ge(sat_staged, j + 1)
                if not isinstance(j, int) or j >= 1:
                    pe.wait_ge(x2t_lo_ready, j)
                    pe.wait_ge(x2t_ready, 2 * j)
                for t in range(TPC):
                    ins = pe.transpose(ps[:, BANK_B, t * P:(t + 1) * P], sat_st[:, t, :], ident[:, :])
                ins.then_inc(satt_psum, 1)

            def out_project(j):
                pe.wait_ge(satt_ready, j + 1)
                for t in range(TPC):
                    ins = pe.matmul(ps[:, BANK_B, t * P:(t + 1) * P], sat_t[:, t * P:(t + 1) * P],
                                    wrd[:, j // (NC // 2), :], start=True, stop=True)
                ins.then_inc(o_psum, 1)

            def x2_transpose(j):
                pe.wait_ge(x2_ready, j + 1)
                for t in range(TPC):
                    ins = pe.transpose(ps[:, BANK_B, t * P:(t + 1) * P], x2[:, t, :], ident[:, :])
                ins.then_inc(x2t_psum, 1)

            def logits(j):
                pe.wait_ge(x2t_ready, 2 * j + 2)
                if not isinstance(j, int) or j >= 1:
                    pe.wait_ge(acc_ready, j)
                for t in range(TPC):
                    ins = pe.matmul(ps[:, BANK_A, t * E:(t + 1) * E], x2_t[:, t * P:(t + 1) * P], wg_sb[:, :],
                                    start=True, stop=True)
                ins.then_inc(logit_psum, 1)

            def gate_transpose(j, par):
                pe.wait_ge(gate_chain, 14 * j + 14)
                for t in range(TPC):
                    ins = pe.transpose(ps[0:E, BANK_A, t * P:(t + 1) * P], gate[par][:, t, :], ident[:, :])
                ins.then_inc(gatet_psum, 1)

            def gates_b2(j):
                pe.wait_ge(gatet_ready, j + 1)
                for t in range(TPC):
                    ins = pe.matmul(ps[:, BANK_A, t * P:(t + 1) * P], gate_t[:, t * P:(t + 1) * P], b2_sb[:, :],
                                    start=True, stop=True)
                ins.then_inc(b2_psum, 1)

            def up(j, par, e, early=False):
                if e == 0:
                    pe.wait_ge(x2t_lo_ready, j + 1)
                for b in range(HB):
                    slot = (2 * e + b) % 4
                    if not (early and e < 2):
                        pe.wait_ge(hid_raw_ready, 16 * j + 2 * e + b - 3)
                    cols = slice((HB * e + b) * P, (HB * e + b + 1) * P)
                    pe.matmul(ps[:, slot, :], w1_pair[:, 0, cols], x2t_hi[:, par, :], start=True, stop=False)
                    pe.matmul(ps[:, slot, :], w1_pair[:, 0, cols], x2t_lo[:, par, :], start=False, stop=False)
                    pe.matmul(ps[:, slot, :], w1_pair[:, 1, cols], x2t_hi[:, par, :], start=False,
                              stop=True).then_inc(up_done, 1)

            def down(j, e, early=False):
                pe.wait_ge(hid_lo_ready, 16 * j + 2 * e + 2)
                if not (early and e < 2):
                    pe.wait_ge(combined, 8 * j + e - 1)
                for t in range(TPC):
                    bank = ps[:, AV0 + e % 2, t * D:(t + 1) * D]
                    for b in range(HB):
                        slot = (2 * e + b) % 4
                        rows = slice(t * P, (t + 1) * P)
                        cols = slice((HB * e + b) * D, (HB * e + b + 1) * D)
                        pe.matmul(bank, hid_hi[:, slot, rows], w2_pair[:, 0, cols], start=(b == 0), stop=False)
                        pe.matmul(bank, hid_hi[:, slot, rows], w2_pair[:, 1, cols], start=False, stop=False)
                        ins = pe.matmul(bank, hid_lo[:, slot, rows], w2_pair[:, 0, cols], start=False, stop=(b == HB - 1))
                ins.then_inc(down_done, 1)

            def ffn(j, par, prep=True, early=False):
                for e in range(E):
                    up(j, par, e, early)
                    if prep and e == 1:
                        sat_transpose(j + 1)
                    if e == 1:
                        gate_transpose(j, par)
                    if prep and e == 2:
                        out_project(j + 1)
                    if e == 3:
                        gates_b2(j)
                    if prep and e == 6:
                        x2_transpose(j + 1)
                    if e >= 1:
                        down(j, e - 1, early)
                    elif not early:
                        down(j - 1, E - 1)
                if prep:
                    logits(j + 1)

            pe.wait_ge(b2_scaled, 1)
            sat_transpose(0)
            out_project(0)
            x2_transpose(0)
            logits(0)
            ffn(0, 0, early=True)
            ffn(1, 1)
            pairs(pe, 2, NC - 2, ffn)
            ffn(NC - 2, 0)
            ffn(NC - 1, 1, prep=False)
            down(NC - 1, E - 1)


INPUTS = ["x", "adj", "L0_gnn_Wq", "L0_gnn_Wk", "L0_gnn_Wv", "L0_gnn_weightr", "L0_gnn_weightd", "L0_gnn_bias",
          "L0_ffn_Wg", "L0_ffn_bg", "L0_ffn_W1", "L0_ffn_b1", "L0_ffn_W2", "L0_ffn_b2"]


def kernel(**inputs):
    import numpy as np
    import concourse.bacc as bacc
    from concourse.bass_utils import run_bass_kernel_spmd

    nc = bacc.Bacc("TRN2", target_bir_lowering=False, num_devices=1)
    arrays, aps = {}, []
    for name in INPUTS:
        a = np.ascontiguousarray(inputs[name])
        arrays[f"in_{name}"] = a
        aps.append(nc.dram_tensor(f"in_{name}", a.shape, mybir.dt.from_np(a.dtype), kind="ExternalInput").ap())
    aps.append(nc.dram_tensor("out", (N, D), F32, kind="ExternalOutput").ap())
    build(nc, *aps)
    r = run_bass_kernel_spmd(nc, [arrays], core_ids=[0])
    return r.results[0]["out"]
```

```python
from contextlib import ExitStack

import concourse.bass as bass
from concourse import mybir

F32 = mybir.dt.float32
F16 = mybir.dt.float16
BF16 = mybir.dt.bfloat16
I32 = mybir.dt.int32
ALU = mybir.AluOpType
ACT = mybir.ActivationFunctionType
AX_X = mybir.AxisListType.X

P = 128
N, D = 4096, 128
HEADS = 2
DH = D // HEADS
SCALE = float(DH) ** -0.5
EPS = 1e-5
SLOPE = 0.01
BIG = 2.0 ** 64
NT = N // P
CH = 512
NC = N // CH
TPC = CH // P
E, H, HB = 8, 256, 2
HALF = N // 2
X_PARTS = 4
X_TILES = NT // X_PARTS
X_CHUNKS = NC // X_PARTS
W_UP = 2.0 ** 8
V_UP = 2.0 ** 5
PIECES = 4
PIECE = N // PIECES

SCORE_BANKS = 2
TR0, TR_BANKS, AV0 = 2, 4, 6
PREP0 = 4
VW = 2 * DH + 2
PT_RING = 4
LAG = 3
POOL_GROUPS = (1, 4, 6)
K_PARTS = ((0, 2), (2, 4), (4, 6), (6, 8))
Q_PARTS = ((0, 4), (4, 8))
POST_STEPS = 3
RANK_STEPS, GATE_STEPS = 11, 14
UP_BANKS = 4
HID_RING = 8
DOWN_LAG = 2
DVE_GROUPS = tuple(g for g in range(NC) if g not in POOL_GROUPS)


def build(nc, x, adj, wq, wk, wv, wr, wd, bias, wg, bg, w1, b1, w2, b2, out):
    with ExitStack() as ctx:
        def sb(name, shape, dt):
            return ctx.enter_context(nc.sbuf_tensor(name, shape, dt))

        def sem(name):
            return ctx.enter_context(nc.semaphore(name))

        ident = sb("ident", [P, P], F32)
        x_sb = sb("x_sb", [P, NT, D], F32)
        mask = sb("mask", [P, 2, N], BF16)
        prob = sb("prob", [P, HEADS, N], F32)
        pt_hi = sb("pt_hi", [P, PT_RING, CH], F16)
        pt_lo = sb("pt_lo", [P, PT_RING, CH], F16)
        pt_raw = sb("pt_raw", [P, len(POOL_GROUPS), CH], F32)
        q_pair = sb("q_pair", [P, HEADS, N], F16)
        k_pair = sb("k_pair", [P, HEADS, N], F16)
        k_swap = sb("k_swap", [P, HEADS, N], F16)
        v_pair = sb("v_pair", [P, NT, HEADS, VW], F16)
        sat = sb("sat", [P, NT, D], F32)
        wq_sb = sb("wq_sb", [P, D], F32)
        wk_sb = sb("wk_sb", [P, D], F32)
        q_lo = sb("q_lo", [P, N], F16)
        wv_sb = sb("wv_sb", [P, D], F32)
        wrd = sb("wrd", [P, 2, D], F32)
        bias_b = sb("bias_b", [P, D], F32)
        wg_sb = sb("wg_sb", [P, E], F32)
        bg_b = sb("bg_b", [P, E], F32)
        b1_sb = sb("b1_sb", [P, E, HB], F32)
        b2_sb = sb("b2_sb", [E, D], F32)
        w1_pair = sb("w1_pair", [P, 2, E * H], F16)
        w2_pair = sb("w2_pair", [P, 2, E * HB * D], F16)
        wg_pair = sb("wg_pair", [P, 2, E], F16)
        b2_pair = sb("b2_pair", [E, 2, D], F16)
        ident16 = sb("ident16", [P, P], F16)
        stats = sb("stats", [P, 8, 6], F32)
        mv = sb("mv", [P, NT, 2], F32)
        ve = sb("ve", [P, NT], F32)
        rstd = sb("rstd", [P, NT], F32)
        expo = sb("expo", [P, NT], F32)
        warm = sb("warm", [P, 1], F32)
        low = sb("low", [P, HEADS, NC], F32)
        nmax = sb("nmax", [P, HEADS], F32)
        rsum = sb("rsum", [P, HEADS], F32)
        av_lo = sb("av_lo", [P, DH], F32)

        def area(h, first, n):
            return prob[:, h, first * CH:(first + n) * CH]

        xn = area(0, 0, 2).rearrange("p (r t d) -> p r t d", r=2, t=TPC)
        xn_t = area(0, 2, 2).rearrange("p (r c) -> p r c", r=2)
        q_hi = area(1, 0, 4).bitcast(F16)
        k_hi, k_lo = [sat[:, i * NT // 2:(i + 1) * NT // 2, :].rearrange("p t d -> p (t d)").bitcast(F16) for i in range(2)]
        w1_raw = area(0, 4, 4)
        w2_raw = area(1, 4, 4)
        hid = prob[:, 1, :].rearrange("p (r c) -> p r c", r=HID_RING)
        hid_hi = area(0, 0, NC // 2).bitcast(F16).rearrange("p (r c) -> p r c", r=HID_RING)
        hid_lo = area(0, NC // 2, NC // 2).bitcast(F16).rearrange("p (r c) -> p r c", r=HID_RING)

        freed = [t[:, h, :].bitcast(F32)[:, c * CH:(c + 1) * CH]
                 for t in (q_pair, k_swap) for h in range(HEADS) for c in range(N // (2 * CH))]
        sat_st, o_pre, o_act, x2, acc0, acc1 = [f.rearrange("p (t d) -> p t d", t=TPC) for f in freed[0:6]]
        acc = [acc0, acc1]
        sat_t = freed[6]
        x2t_hi = freed[8].bitcast(F16).rearrange("p (r c) -> p r c", r=2)
        x2t_lo = freed[9].bitcast(F16).rearrange("p (r c) -> p r c", r=2)
        gate_t = freed[10].bitcast(F16)[0:E, 0:CH]
        small = freed[11]
        fields = [small[:, 32 * k:32 * (k + 1)].rearrange("p (t e) -> p t e", e=E) for k in range(9)]
        logit, top8, above, tied, rank, keep, chosen, gate0, gate1 = fields
        gate = [gate0, gate1]
        gate16 = small[:, 288:304].bitcast(F16).rearrange("p (t e) -> p t e", e=E)
        mv2 = small[:, 304:312].rearrange("p (t s) -> p t s", s=2)
        ve2, rstd2 = small[:, 312:316], small[:, 316:320]

        ps = ctx.enter_context(nc.psum_tensor("ps", [P, 8, CH], F32))

        x_in = [sem(f"x_in{i}") for i in range(X_PARTS)]
        qkv_w_in = sem("qkv_w_in")
        w_in = sem("w_in")
        w1_in = sem("w1_in")
        w2_in = sem("w2_in")
        b1_in = sem("b1_in")
        w_split_chain = sem("w_split_chain")
        adj_in = [sem(f"adj_in{q}") for q in range(2)]
        q_in = [sem(f"q_in{n}") for n in range(len(Q_PARTS))]
        k_in = [[sem(f"k_in{n}_{h}") for h in range(HEADS)] for n in range(len(K_PARTS))]
        out_done = [sem(f"out_done{r}") for r in range(2)]
        ident_zero = sem("ident_zero")
        ident_ready = sem("ident_ready")
        ones_ready = sem("ones_ready")
        mask_ready = sem("mask_ready")
        stats_chain = sem("stats_chain")
        var_ready = sem("var_ready")
        rstd_ready = sem("rstd_ready")
        xn_ready = sem("xn_ready")
        xnt_psum = sem("xnt_psum")
        xnt_ready = sem("xnt_ready")
        proj_psum = sem("proj_psum")
        hi_ready = sem("hi_ready")
        lo_ready = sem("lo_ready")
        v_psum = sem("v_psum")
        v_hi_ready = sem("v_hi_ready")
        v_lo_ready = sem("v_lo_ready")
        scores_ready = sem("scores_ready")
        masked = sem("masked")
        max_ready = sem("max_ready")
        exp_done = sem("exp_done")
        transposed = sem("transposed")
        pt_hi_ready = sem("pt_hi_ready")
        pt_raw_ready = sem("pt_raw_ready")
        pt_pool_hi = sem("pt_pool_hi")
        pt_by_dve = sem("pt_by_dve")
        pt_by_pool = sem("pt_by_pool")
        av_done = sem("av_done")
        sum_inv = sem("sum_inv")
        av_lo_ready = sem("av_lo_ready")
        sat_ready = sem("sat_ready")
        sat_staged = sem("sat_staged")
        satt_psum = sem("satt_psum")
        satt_ready = sem("satt_ready")
        o_psum = sem("o_psum")
        post_chain = sem("post_chain")
        ve2_ready = sem("ve2_ready")
        rstd2_ready = sem("rstd2_ready")
        x2_ready = sem("x2_ready")
        x2t_psum = sem("x2t_psum")
        x2t_ready = sem("x2t_ready")
        x2t_lo_ready = sem("x2t_lo_ready")
        logit_psum = sem("logit_psum")
        gate_chain = sem("gate_chain")
        gatet_psum = sem("gatet_psum")
        gatet_ready = sem("gatet_ready")
        b2_psum = sem("b2_psum")
        acc_ready = sem("acc_ready")
        up_done = sem("up_done")
        hid_raw_ready = sem("hid_raw_ready")
        hid_hi_ready = sem("hid_hi_ready")
        hid_lo_ready = sem("hid_lo_ready")
        down_done = sem("down_done")
        combined = sem("combined")

        def pairs(eng, first, end, body):
            with eng.Fori(0, (end - first) // 2) as k:
                body(2 * k + first, first % 2)
                body(2 * k + first + 1, (first + 1) % 2)

        def wait_pt(eng, unit, g):
            if g in POOL_GROUPS:
                eng.wait_ge(pt_by_pool, len(POOL_GROUPS) * unit + POOL_GROUPS.index(g) + 1)
            else:
                eng.wait_ge(pt_by_dve, len(DVE_GROUPS) * unit + DVE_GROUPS.index(g) + 1)

        block = ctx.enter_context(nc.Block())
        N_QKV_W, N_W = 3, 6
        W_SPLITS = 13

        @block.sync
        def _(sp):
            xv = x.rearrange("(t p) d -> p t d", p=P)
            for i in range(X_PARTS):
                part = slice(i * X_TILES, (i + 1) * X_TILES)
                sp.dma_start(x_sb[:, part, :], xv[:, part, :]).then_inc(x_in[i], 16)

            sp.dma_start(wg_sb[:, :], wg).then_inc(w_in, 16)
            sp.dma_start(b2_sb[:, :], b2).then_inc(w_in, 16)
            sp.dma_start(w1_raw.rearrange("p (e h) -> p e h", e=E), w1.rearrange("e d h -> d e h")).then_inc(w1_in, 16)
            sp.dma_start(w2_raw.rearrange("p (e b d) -> p e b d", e=E, b=HB),
                         w2.rearrange("e (b p) d -> p e b d", b=HB)).then_inc(w2_in, 16)
            sp.dma_start(wrd[:, 0, :], wr).then_inc(w_in, 16)
            sp.dma_start(wrd[:, 1, :], wd).then_inc(w_in, 16)
            sp.dma_start(bias_b[:, :], bias.rearrange("(a d) -> a d", a=1).to_broadcast([P, D])).then_inc(w_in, 16)
            sp.dma_start(bg_b[:, :], bg.rearrange("(a d) -> a d", a=1).to_broadcast([P, E])).then_inc(w_in, 16)
            with nc.allow_non_contiguous_dma(reason="2048 values, once"):
                sp.dma_start(b1_sb[:, :, :], b1.rearrange("e (b p) -> p e b", p=P)).then_inc(b1_in, 16)
            for part, (c0, c1) in enumerate(K_PARTS):
                sp.wait_ge(lo_ready, 2 * c1)
                sp.wait_ge(hi_ready, 2 * c1)
                cols = slice(c0 * CH, c1 * CH)
                for h in range(HEADS):
                    head = slice(h * DH, (h + 1) * DH)
                    for dst, top, bottom in ((k_pair, k_hi, k_lo), (k_swap, k_lo, k_hi)):
                        sp.dma_start(dst[0:DH, h, cols], top[head, cols]).then_inc(k_in[part][h], 16)
                        sp.dma_start(dst[DH:P, h, cols], bottom[head, cols]).then_inc(k_in[part][h], 16)
            ov = out.rearrange("(t p) d -> p t d", p=P)

            def store(j, par):
                sp.wait_ge(combined, E * j + E)
                sp.dma_start(ov[:, bass.ds(j * TPC, TPC), :], acc[par]).then_inc(out_done[par], 16)

            pairs(sp, 0, NC, store)
            for r in range(2):
                sp.wait_ge(out_done[r], 16 * NC // 2)

        @block.gpsimd
        def _(pool):
            pool.memset(ident[:, :], 0.0).then_inc(ident_zero, 1)
            pool.wait_ge(ident_zero, 1)
            pool.affine_select(out=ident[:, :], in_=ident[:, :], compare_op=ALU.not_equal, fill=1.0, base=0,
                               pattern=[[-1, P]], channel_multiplier=1).then_inc(ident_ready, 1)
            pool.memset(v_pair[:, :, :, DH:DH + 1], V_UP).then_inc(ones_ready, 1)

            pool.memset(expo[:, :], -0.5).then_inc(ones_ready, 1)

            def load_adj(i, par):
                if not isinstance(i, int) or i >= 2:
                    pool.wait_ge(masked, 16 * (i - 2) + 16)
                pool.dma_start(mask[:, par, :], adj[bass.ds(i * P, P), :], max_dma_last_dim=8192).then_inc(adj_in[par], 16)

            def inverse_std_x(i):
                part = slice(i * X_TILES, (i + 1) * X_TILES)
                pool.wait_ge(var_ready, i + 1)
                pool.tensor_tensor(rstd[:, part], ve[:, part], expo[:, part], ALU.pow).then_inc(rstd_ready, 1)

            def split_weights(n, raw, pair):
                pool.tensor_scalar(raw, raw, W_UP, 0.0, ALU.mult, ALU.add).then_inc(w_split_chain, 1)
                pool.wait_ge(w_split_chain, 3 * n + 1)
                pool.tensor_scalar(pair[:, 0, :], raw, 1.0, 0.0, ALU.mult, ALU.add).then_inc(w_split_chain, 1)
                pool.wait_ge(w_split_chain, 3 * n + 2)
                pool.tensor_tensor(pair[:, 1, :], raw, pair[:, 0, :], ALU.subtract).then_inc(w_split_chain, 1)

            def place_q(part):
                c0, c1 = Q_PARTS[part]
                pool.wait_ge(lo_ready, 2 * c1)
                pool.wait_ge(hi_ready, 2 * c1)
                cols = slice(c0 * CH, c1 * CH)
                for h in range(HEADS):
                    head = slice(h * DH, (h + 1) * DH)
                    pool.dma_start(q_pair[0:DH, h, cols], q_hi[head, cols]).then_inc(q_in[part], 16)
                    pool.dma_start(q_pair[DH:P, h, cols], q_lo[head, cols]).then_inc(q_in[part], 16)

            pool.wait_ge(ones_ready, 2)
            for i in range(X_PARTS):
                inverse_std_x(i)
            load_adj(0, 0)
            load_adj(1, 1)
            pool.wait_ge(w1_in, 16)
            split_weights(0, w1_raw, w1_pair)
            place_q(0)
            pool.wait_ge(w2_in, 16)
            split_weights(1, w2_raw, w2_pair)
            place_q(1)
            pool.wait_ge(w_in, 16 * N_W)
            split_weights(2, wg_sb[:, :], wg_pair)
            split_weights(3, b2_sb[:, :], b2_pair)
            pool.tensor_scalar(ident16[:, :], ident[:, :], 1.0, 0.0, ALU.mult, ALU.add).then_inc(w_split_chain, 1)

            def inverse_std(j):
                pool.wait_ge(ve2_ready, j + 1)
                pool.tensor_tensor(rstd2, ve2, expo[:, 0:TPC], ALU.pow).then_inc(rstd2_ready, 1)

            def split_pt(j, h, k):
                g = POOL_GROUPS[k]
                count = len(POOL_GROUPS) * (2 * j + h) + k + 1
                pool.wait_ge(pt_raw_ready, count)
                pool.nop(nofuse=True)
                pool.tensor_scalar(pt_hi[:, g % PT_RING, :], pt_raw[:, k, :], 1.0, 0.0, ALU.mult,
                                   ALU.add).then_inc(pt_pool_hi, 1)
                pool.wait_ge(pt_pool_hi, count)
                pool.tensor_tensor(pt_lo[:, g % PT_RING, :], pt_raw[:, k, :], pt_hi[:, g % PT_RING, :],
                                   ALU.subtract).then_inc(pt_by_pool, 1)

            def step(i, par, ahead=True, last=False):
                if ahead:
                    load_adj(i + 1, 1 - par)
                for h in range(HEADS):
                    for k in range(len(POOL_GROUPS)):
                        split_pt(i - 1, h, k)
                    if last and h == 0:
                        inverse_std(0)

            step(1, 1)
            pairs(pool, 2, NT - 2, step)
            step(NT - 2, 0)
            step(NT - 1, 1, ahead=False)
            step(NT, 0, ahead=False, last=True)

            def ffn(j, par, prep=True):
                for e in range(E):
                    for b in range(HB):
                        slot = (2 * e + b) % HID_RING
                        pool.wait_ge(hid_hi_ready, 16 * j + 2 * e + b + 1)
                        pool.tensor_tensor(hid_lo[:, slot, :], hid[:, slot, :], hid_hi[:, slot, :],
                                           ALU.subtract).then_inc(hid_lo_ready, 1)
                    if prep and e == 3:
                        inverse_std(j + 1)

            pairs(pool, 0, NC - 2, ffn)
            ffn(NC - 2, 0)
            ffn(NC - 1, 1, prep=False)

        @block.scalar
        def _(act):
            act.dma_start(wq_sb[:, :], wq).then_inc(qkv_w_in, 16)
            act.dma_start(wk_sb[:, :], wk).then_inc(qkv_w_in, 16)
            act.dma_start(wv_sb[:, :], wv).then_inc(qkv_w_in, 16)

            def copy_xnt(j, par):
                act.wait_ge(xnt_psum, j + 1)
                act.activation(xn_t[:, par, :], ps[:, PREP0 + par, :], ACT.Copy).then_inc(xnt_ready, 1)

            def project(j, par, ahead=True):
                cols = bass.ds(j * CH, CH)
                for m, (dst, scale) in enumerate(((q_hi, SCALE), (k_hi, 1.0))):
                    act.wait_ge(proj_psum, 2 * j + m + 1)
                    act.activation(dst[:, cols], ps[:, 2 * par + m, :], ACT.Copy, scale=scale).then_inc(hi_ready, 1)
                act.wait_ge(v_psum, j + 1)
                act.activation(v_pair[:, bass.ds(j * TPC, TPC), :, 0:DH],
                               ps[:, AV0 + par, :].rearrange("p (t h c) -> p t h c", t=TPC, h=HEADS),
                               ACT.Copy, scale=V_UP).then_inc(v_hi_ready, 1)
                if ahead:
                    copy_xnt(j + 2, par)

            copy_xnt(0, 0)
            copy_xnt(1, 1)
            project(0, 0)
            project(1, 1)
            pairs(act, 2, NC - 2, project)
            project(NC - 2, 0, ahead=False)
            project(NC - 1, 1, ahead=False)

            def exp_piece(j, h, n):
                if n == 0:
                    act.wait_ge(max_ready, 2 * j + h + 1)
                cols = slice(n * PIECE, (n + 1) * PIECE)
                act.activation(prob[:, h, cols], prob[:, h, cols], ACT.Exp, bias=nmax[:, h:h + 1],
                               scale=-1.0).then_inc(exp_done, 1)

            def split_pt(j, h, g, early=False):
                act.wait_ge(transposed, 16 * j + 8 * h + g + 1)
                if not (early and h == 0 and g < PT_RING):
                    act.wait_ge(av_done, 16 * j + 8 * h + g - PT_RING + 1)
                if g in POOL_GROUPS:
                    act.activation(pt_raw[:, POOL_GROUPS.index(g), :], ps[:, TR0 + g % TR_BANKS, :],
                                   ACT.Copy).then_inc(pt_raw_ready, 1)
                else:
                    act.activation(pt_hi[:, g % PT_RING, :], ps[:, TR0 + g % TR_BANKS, :],
                                   ACT.Copy).then_inc(pt_hi_ready, 1)

            def satt_copy(j, bank=PREP0 + 1):
                act.wait_ge(satt_psum, j + 1)
                act.activation(sat_t, ps[:, bank, :], ACT.Copy).then_inc(satt_ready, 1)

            def x2t_high(j, par, bank=PREP0 + 1):
                act.wait_ge(x2t_psum, j + 1)
                act.activation(x2t_hi[:, par, :], ps[:, bank, :], ACT.Copy).then_inc(x2t_ready, 1)

            def step(i, prior=True, now=True, early=False, last=False):
                for h in range(HEADS):
                    has_exp = prior if h == 0 else now
                    ej, eh = (i - 1, 1) if h == 0 else (i, 0)
                    for g in range(NC):
                        if prior:
                            split_pt(i - 1, h, g, early)
                        if has_exp and g % 2 == 1:
                            exp_piece(ej, eh, g // 2)
                        if last and (h, g) == (0, 2):
                            satt_copy(0, bank=1)
                        if last and (h, g) == (0, 7):
                            act.activation(warm[:, :], expo[:, 0:1], ACT.Gelu)
                        if last and (h, g) == (1, 5):
                            x2t_high(0, 0, bank=1)

            step(0, prior=False)
            step(1, early=True)
            pairs(act, 2, NT, lambda i, par: step(i))
            step(NT, now=False, last=True)

            act.wait_ge(b1_in, 16)

            def gatet_copy(j):
                act.wait_ge(gatet_psum, j + 1)
                act.activation(gate_t, ps[0:E, PREP0, 0:CH // 2].bitcast(F16), ACT.Copy).then_inc(gatet_ready, 1)

            def ffn(j, par, prep=True, early=False):
                for e in range(E):
                    for b in range(HB):
                        slot = (2 * e + b) % HID_RING
                        act.wait_ge(up_done, 16 * j + 2 * e + b + 1)
                        if not (early and e < HID_RING // HB):
                            act.wait_ge(down_done, 8 * j + e - 3)
                        act.activation(hid[:, slot, :], ps[:, (2 * e + b) % UP_BANKS, :], ACT.Gelu, bias=b1_sb[:, e, b:b + 1],
                                       scale=1.0 / W_UP).then_inc(hid_raw_ready, 1)
                        act.wait_ge(hid_raw_ready, 16 * j + 2 * e + b + 1)
                        act.activation(hid_hi[:, slot, :], hid[:, slot, :], ACT.Copy).then_inc(hid_hi_ready, 1)
                    if prep and e == 1:
                        satt_copy(j + 1)
                    if e == 3:
                        gatet_copy(j)
                    if prep and e == 6:
                        x2t_high(j + 1, 1 - par)

            ffn(0, 0, early=True)
            ffn(1, 1)
            pairs(act, 2, NC - 2, ffn)
            ffn(NC - 2, 0)
            ffn(NC - 1, 1, prep=False)

        @block.vector
        def _(dve):
            def linker(s, base):
                count = [base]

                def link(ins):
                    count[0] = count[0] + 1
                    ins.then_inc(s, 1)
                    dve.wait_ge(s, count[0])
                return link

            def settled():
                dve.nop(nofuse=True)

            def row_statistics(i):
                dve.wait_ge(x_in[i], 16)
                for t in range(X_TILES):
                    ins = dve.bn_stats(stats[:, t, :], x_sb[:, X_TILES * i + t, :])
                ins.then_inc(stats_chain, 1)
                dve.wait_ge(stats_chain, 2 * i + 1)
                for t in range(X_TILES):
                    ins = dve.bn_aggr(mv[:, X_TILES * i + t, :], stats[:, t, :])
                ins.then_inc(stats_chain, 1)
                dve.wait_ge(stats_chain, 2 * i + 2)
                part = slice(i * X_TILES, (i + 1) * X_TILES)
                dve.tensor_scalar(ve[:, part], mv[:, part, 1], EPS, None, ALU.add).then_inc(var_ready, 1)

            def normalise_x(j, par):
                for t in range(TPC):
                    tile = j * TPC + t
                    ins = dve.tensor_scalar(xn[:, par, t, :], x_sb[:, tile, :], mv[:, tile, 0:1],
                                            rstd[:, bass.ds(tile, 1)], ALU.subtract, ALU.mult)
                ins.then_inc(xn_ready, 1)

            def project(j, par, ahead=True):
                if ahead:
                    dve.wait_ge(xnt_psum, j + 1)
                    dve.wait_ge(rstd_ready, (j + 2) // X_CHUNKS + 1)
                    normalise_x(j + 2, par)
                cols = bass.ds(j * CH, CH)
                for m, (lo, hi, scale) in enumerate(((q_lo, q_hi, SCALE), (k_lo, k_hi, 1.0))):
                    dve.wait_ge(hi_ready, 2 * j + m + 1)
                    dve.scalar_tensor_tensor(lo[:, cols], ps[:, 2 * par + m, :], scale, hi[:, cols], ALU.mult,
                                             ALU.subtract).then_inc(lo_ready, 1)
                dve.wait_ge(v_hi_ready, j + 1)
                tiles = bass.ds(j * TPC, TPC)
                dve.scalar_tensor_tensor(v_pair[:, tiles, :, DH + 1:2 * DH + 1],
                                         ps[:, AV0 + par, :].rearrange("p (t h c) -> p t h c", t=TPC, h=HEADS), V_UP,
                                         v_pair[:, tiles, :, 0:DH], ALU.mult, ALU.subtract).then_inc(v_lo_ready, 1)

            def make_mask(i, par, half):
                dve.wait_ge(adj_in[par], 8 * i - 8 * par + 16)
                part = mask[:, par, half * HALF:(half + 1) * HALF]
                dve.tensor_scalar(part, part, 0.0, -BIG, ALU.is_le, ALU.mult).then_inc(mask_ready, 1)

            row_statistics(0)
            row_statistics(1)
            dve.wait_ge(rstd_ready, 1)
            normalise_x(0, 0)
            normalise_x(1, 1)
            row_statistics(2)
            row_statistics(3)
            project(0, 0)
            project(1, 1)
            pairs(dve, 2, NC - 2, project)
            make_mask(0, 0, 0)
            project(NC - 2, 0, ahead=False)
            make_mask(0, 0, 1)
            project(NC - 1, 1, ahead=False)

            def mask_scores(i, par, h, c):
                if c == 0:
                    dve.wait_ge(mask_ready, 2 * i + 2)
                if isinstance(i, int) and i == 0 and c == 0:
                    dve.wait_ge(w_split_chain, 3 * (h + 1))
                    if h == 1:
                        for s in q_in:
                            dve.wait_ge(s, 64)
                dve.wait_ge(scores_ready, 16 * i + 8 * h + c + 1)
                cols = slice(c * CH, (c + 1) * CH)
                settled()
                dve.tensor_tensor_reduce(out=prob[:, h, cols], in0=ps[:, c % SCORE_BANKS, :], in1=mask[:, par, cols],
                                         scale=-1.0, scalar=3.0e38, op0=ALU.add, op1=ALU.min,
                                         accum_out=low[:, h, c:c + 1]).then_inc(masked, 1)

            def split_pt(j, h, g):
                dve.wait_ge(pt_hi_ready, len(DVE_GROUPS) * (2 * j + h) + DVE_GROUPS.index(g) + 1)
                dve.tensor_tensor(pt_lo[:, g % PT_RING, :], ps[:, TR0 + g % TR_BANKS, :], pt_hi[:, g % PT_RING, :],
                                  ALU.subtract).then_inc(pt_by_dve, 1)

            def finish_head(j, h):
                acc_h = ps[:, AV0 + h, :]
                dve.wait_ge(av_done, 16 * j + 8 * h + 8)
                dve.reciprocal(rsum[:, h:h + 1], acc_h[:, DH:DH + 1]).then_inc(sum_inv, 1)
                dve.wait_ge(sum_inv, 2 * j + h + 1)
                dve.tensor_scalar(av_lo[:, :], acc_h[:, DH + 1:2 * DH + 1], rsum[:, h:h + 1], None,
                                  ALU.mult).then_inc(av_lo_ready, 1)
                dve.wait_ge(av_lo_ready, 2 * j + h + 1)
                dve.scalar_tensor_tensor(sat[:, j, h * DH:(h + 1) * DH], acc_h[:, 0:DH], rsum[:, h:h + 1], av_lo[:, :],
                                         ALU.mult, ALU.add).then_inc(sat_ready, 1)

            def stage_sat(j):
                if not isinstance(j, int) or j >= 1:
                    dve.wait_ge(satt_psum, j)
                dve.tensor_copy(sat_st, sat[:, bass.ds(j * TPC, TPC), :]).then_inc(sat_staged, 1)

            def residual(j, par, bank=PREP0 + 1):
                link = linker(post_chain, POST_STEPS * j)
                dve.wait_ge(o_psum, j + 1)
                link(dve.tensor_tensor(o_pre, ps[:, bank, :].rearrange("p (t d) -> p t d", d=D),
                                       bias_b[:, :].unsqueeze(1).to_broadcast([P, TPC, D]), ALU.add))
                link(dve.scalar_tensor_tensor(o_act, o_pre, SLOPE, o_pre, ALU.mult, ALU.max))
                if not isinstance(j, int) or j >= 2:
                    dve.wait_ge(out_done[par], 8 * j - 8 * par)
                link(dve.tensor_tensor(acc[par], x_sb[:, bass.ds(j * TPC, TPC), :], o_act, ALU.add))

            def statistics(j, par):
                settled()
                for t in range(TPC):
                    ins = dve.bn_stats(stats[:, t, :], acc[par][:, t, :])
                ins.then_inc(stats_chain, 1)
                dve.wait_ge(stats_chain, 2 * X_PARTS + 2 * j + 1)
                settled()
                for t in range(TPC):
                    ins = dve.bn_aggr(mv2[:, t, :], stats[:, t, :])
                ins.then_inc(stats_chain, 1)
                dve.wait_ge(stats_chain, 2 * X_PARTS + 2 * j + 2)
                dve.tensor_scalar(ve2, mv2[:, :, 1], EPS, None, ALU.add).then_inc(ve2_ready, 1)

            def normalise(j, par):
                dve.wait_ge(rstd2_ready, j + 1)
                for t in range(TPC):
                    ins = dve.tensor_scalar(x2[:, t, :], acc[par][:, t, :], mv2[:, t, 0:1], rstd2[:, t:t + 1],
                                            ALU.subtract, ALU.mult)
                ins.then_inc(x2_ready, 1)

            def x2t_low(j, par, bank=PREP0 + 1):
                dve.wait_ge(x2t_ready, j + 1)
                dve.tensor_tensor(x2t_lo[:, par, :], ps[:, bank, :], x2t_hi[:, par, :],
                                  ALU.subtract).then_inc(x2t_lo_ready, 1)

            def rank_gates(j, bank=PREP0):
                link = linker(gate_chain, GATE_STEPS * j)
                dve.wait_ge(logit_psum, j + 1)
                link(dve.scalar_tensor_tensor(logit, ps[:, bank, 0:TPC * E].rearrange("p (t e) -> p t e", e=E),
                                              1.0 / W_UP, bg_b[:, :].unsqueeze(1).to_broadcast([P, TPC, E]),
                                              ALU.mult, ALU.add))
                settled()
                for t in range(TPC):
                    ins = dve.max(top8[:, t, :], logit[:, t, :])
                link(ins)
                second = top8[:, :, 1:2].to_broadcast([P, TPC, E])
                dve.tensor_tensor(above, logit, second, ALU.is_gt)
                link(dve.tensor_tensor(tied, logit, second, ALU.is_equal))
                link(dve.tensor_reduce(rank[:, :, 0:1], above, AX_X, ALU.add))
                for e in range(1, E):
                    link(dve.tensor_tensor(rank[:, :, e:e + 1], rank[:, :, e - 1:e], tied[:, :, e - 1:e], ALU.add))

            def choose_gates(j, par):
                link = linker(gate_chain, GATE_STEPS * j + RANK_STEPS)
                link(dve.scalar_tensor_tensor(keep, rank, 2.0, tied, ALU.is_lt, ALU.mult))
                link(dve.tensor_tensor(chosen, keep, above, ALU.add))
                dve.tensor_scalar(gate[par], chosen, 1.0 / W_UP, None, ALU.mult)
                link(dve.tensor_scalar(gate16, chosen, 1.0 / W_UP, None, ALU.mult))

            def step(i, par, prior=True, now=True, post=True, ahead=True, last=False):
                for h in range(HEADS):
                    for c in range(NC):
                        if now:
                            mask_scores(i, par, h, c)
                        if prior and c in DVE_GROUPS:
                            split_pt(i - 1, h, c)
                        if c == 4 and h == 0 and post:
                            finish_head(i - 2, 1)
                        if c == 4 and h == 1 and prior:
                            finish_head(i - 1, 0)
                        if ahead and h == 1 and c in (1, 6):
                            make_mask(i + 1, 1 - par, c // 6)
                        if last and (h, c) == (0, 5):
                            residual(0, 0, bank=1)
                            stage_sat(1)
                            statistics(0, 0)
                        if last and (h, c) == (1, 1):
                            normalise(0, 0)
                        if last and (h, c) == (1, 7):
                            x2t_low(0, 0, bank=1)
                    if now:
                        dve.wait_ge(masked, 16 * i + 8 * h + 8)
                        dve.tensor_reduce(nmax[:, h:h + 1], low[:, h, :], AX_X, ALU.min).then_inc(max_ready, 1)

            step(0, 0, prior=False, post=False)
            step(1, 1, post=False)
            pairs(dve, 2, NT - 2, step)
            step(NT - 2, 0)
            step(NT - 1, 1, ahead=False)
            dve.wait_ge(w_in, 16 * N_W)
            stage_sat(0)
            step(NT, 0, now=False, ahead=False, last=True)
            rank_gates(0, bank=0)
            finish_head(NT - 1, 1)
            choose_gates(0, 0)

            def add_b2(j, par):
                dve.wait_ge(b2_psum, j + 1)
                dve.wait_ge(combined, 8 * j + 3)
                dve.tensor_tensor(acc[par], ps[:, PREP0, :].rearrange("p (t d) -> p t d", d=D), acc[par],
                                  ALU.add).then_inc(acc_ready, 1)

            def combine(j, par, e):
                dve.wait_ge(down_done, 8 * j + e + 1)
                if e == 0:
                    dve.wait_ge(gate_chain, GATE_STEPS * (j + 1))
                elif e == 3:
                    dve.wait_ge(acc_ready, j + 1)
                else:
                    dve.wait_ge(combined, 8 * j + e)
                for t in range(TPC):
                    ins = dve.scalar_tensor_tensor(acc[par][:, t, :], ps[:, AV0 + e % 2, t * D:(t + 1) * D],
                                                   gate[par][:, t, e:e + 1], acc[par][:, t, :], ALU.mult, ALU.add)
                ins.then_inc(combined, 1)

            def ffn(j, par, prep=True, stage=True):
                for e in range(E):
                    combine(j, par, e)
                    if prep and e == 0:
                        residual(j + 1, 1 - par)
                        statistics(j + 1, 1 - par)
                    if e == 2:
                        add_b2(j, par)
                    if prep and e == 3:
                        normalise(j + 1, 1 - par)
                    if stage and e == 4:
                        stage_sat(j + 2)
                    if prep and e == 4:
                        x2t_low(j + 1, 1 - par)
                    if prep and e == 5:
                        rank_gates(j + 1)
                    if prep and e == 6:
                        choose_gates(j + 1, 1 - par)

            ffn(0, 0)
            ffn(1, 1)
            pairs(dve, 2, NC - 2, ffn)
            ffn(NC - 2, 0, stage=False)
            ffn(NC - 1, 1, prep=False, stage=False)

        @block.tensor
        def _(pe):
            def transpose_x(j, par):
                pe.wait_ge(xn_ready, j + 1)
                for t in range(TPC):
                    ins = pe.transpose(ps[:, PREP0 + par, t * P:(t + 1) * P], xn[:, par, t, :], ident[:, :])
                ins.then_inc(xnt_psum, 1)

            def project(j, par, ahead=True):
                pe.wait_ge(xnt_ready, j + 1)
                for m, w in enumerate((wq_sb, wk_sb)):
                    if not isinstance(j, int) or j >= 2:
                        pe.wait_ge(lo_ready, 2 * (j - 2) + m + 1)
                    pe.matmul(ps[:, 2 * par + m, :], w[:, :], xn_t[:, par, :], start=True,
                              stop=True).then_inc(proj_psum, 1)
                if not isinstance(j, int) or j >= 2:
                    pe.wait_ge(v_lo_ready, j - 1)
                for t in range(TPC):
                    ins = pe.matmul(ps[:, AV0 + par, t * P:(t + 1) * P], xn_t[:, par, t * P:(t + 1) * P], wv_sb[:, :],
                                    start=True, stop=True)
                ins.then_inc(v_psum, 1)
                if ahead:
                    transpose_x(j + 2, par)

            pe.wait_ge(ident_ready, 1)
            transpose_x(0, 0)
            transpose_x(1, 1)
            pe.wait_ge(qkv_w_in, 16 * N_QKV_W)
            project(0, 0)
            project(1, 1)
            pairs(pe, 2, NC - 2, project)
            project(NC - 2, 0, ahead=False)
            project(NC - 1, 1, ahead=False)
            pe.wait_ge(lo_ready, 2 * (NC - 1))

            def scores(i, h, c):
                if not (isinstance(i, int) and i == 0 and h == 0 and c < SCORE_BANKS):
                    pe.wait_ge(masked, 16 * i + 8 * h + c - SCORE_BANKS + 1)
                if isinstance(i, int) and i == 0:
                    for part, (c0, _) in enumerate(K_PARTS):
                        if c == c0:
                            pe.wait_ge(k_in[part][h], 64)
                    if h == 0 and c == 0:
                        pe.wait_ge(q_in[0], 64)
                q = q_pair[:, h, bass.ds(i * P, P)]
                cols = slice(c * CH, (c + 1) * CH)
                bank = ps[:, c % SCORE_BANKS, :]
                pe.matmul(bank, q, k_pair[:, h, cols], start=True, stop=False)
                pe.matmul(bank, q, k_swap[:, h, cols], start=False, stop=True).then_inc(scores_ready, 1)

            def transposes(j, h, g):
                if g % 2 == 0:
                    pe.wait_ge(exp_done, PIECES * (2 * j + h) + g // 2 + 1)
                for t in range(TPC):
                    ins = pe.transpose(ps[:, TR0 + g % TR_BANKS, t * P:(t + 1) * P],
                                       prob[:, h, g * CH + t * P:g * CH + (t + 1) * P], ident[:, :])
                ins.then_inc(transposed, 1)

            def attend(j, h, g, first=False):
                wait_pt(pe, 2 * j + h, g)
                if g == 0 and not first:
                    pe.wait_ge(sat_ready, 2 * (j - 1) + h + 1)
                for t in range(TPC):
                    tile = g * TPC + t
                    pe.matmul(ps[:, AV0 + h, 0:2 * DH + 1], pt_hi[:, g % PT_RING, t * P:(t + 1) * P],
                              v_pair[:, tile, h, 0:2 * DH + 1], start=(tile == 0), stop=False)
                    ins = pe.matmul(ps[:, AV0 + h, 0:DH + 1], pt_lo[:, g % PT_RING, t * P:(t + 1) * P],
                                    v_pair[:, tile, h, 0:DH + 1], start=False, stop=(tile == NT - 1))
                ins.then_inc(av_done, 1)

            BANK_A, BANK_B = PREP0, PREP0 + 1

            def sat_transpose(j, bank=BANK_B):
                pe.wait_ge(sat_staged, j + 1)
                if not isinstance(j, int) or j >= 1:
                    pe.wait_ge(x2t_lo_ready, j)
                for t in range(TPC):
                    ins = pe.transpose(ps[:, bank, t * P:(t + 1) * P], sat_st[:, t, :], ident[:, :])
                ins.then_inc(satt_psum, 1)

            def out_project(j, bank=BANK_B):
                pe.wait_ge(satt_ready, j + 1)
                for t in range(TPC):
                    ins = pe.matmul(ps[:, bank, t * P:(t + 1) * P], sat_t[:, t * P:(t + 1) * P],
                                    wrd[:, j // (NC // 2), :], start=True, stop=True)
                ins.then_inc(o_psum, 1)

            def x2_transpose(j, bank=BANK_B):
                pe.wait_ge(x2_ready, j + 1)
                for t in range(TPC):
                    ins = pe.transpose(ps[:, bank, t * P:(t + 1) * P], x2[:, t, :], ident[:, :])
                ins.then_inc(x2t_psum, 1)

            def logits(j, par, bank=BANK_A):
                pe.wait_ge(x2t_lo_ready, j + 1)
                if not isinstance(j, int) or j >= 1:
                    pe.wait_ge(acc_ready, j)
                for t in range(TPC):
                    rows = slice(t * P, (t + 1) * P)
                    scores_t = ps[:, bank, t * E:(t + 1) * E]
                    pe.matmul(scores_t, x2t_hi[:, par, rows], wg_pair[:, 0, :], start=True, stop=False)
                    pe.matmul(scores_t, x2t_hi[:, par, rows], wg_pair[:, 1, :], start=False, stop=False)
                    ins = pe.matmul(scores_t, x2t_lo[:, par, rows], wg_pair[:, 0, :], start=False, stop=True)
                ins.then_inc(logit_psum, 1)

            def step(i, par, prior=True, now=True, post=True, early=False, last=False):
                def attend_behind(h, g):
                    if prior and g >= LAG:
                        attend(i - 1, h, g - LAG, early)
                    elif prior and h == 1:
                        attend(i - 1, 0, g + NC - LAG)
                    elif prior and post:
                        attend(i - 2, 1, g + NC - LAG)

                for h in range(HEADS):
                    for g in range(NC):
                        if g % 2 == 0:
                            attend_behind(h, g)
                        if prior:
                            transposes(i - 1, h, g)
                        if g % 2 == 1:
                            if now:
                                scores(i, h, g - 1)
                            attend_behind(h, g)
                            if now:
                                scores(i, h, g)
                        if last and (h, g) == (0, 1):
                            sat_transpose(0, bank=1)
                        if last and (h, g) == (0, 4):
                            out_project(0, bank=1)
                        if last and (h, g) == (1, 4):
                            x2_transpose(0, bank=1)

            step(0, 0, prior=False, post=False)
            pe.wait_ge(v_lo_ready, NC)
            pe.wait_ge(ones_ready, 2)
            pe.wait_ge(q_in[1], 64)
            pe.wait_ge(w_in, 16 * N_W)
            step(1, 1, post=False, early=True)
            pairs(pe, 2, NT, step)
            step(NT, 0, now=False, last=True)
            for g in range(NC - LAG, NC):
                attend(NT - 1, 1, g)
            pe.wait_ge(w_split_chain, W_SPLITS)
            logits(0, 0, bank=0)

            def gate_transpose(j):
                pe.wait_ge(gate_chain, GATE_STEPS * (j + 1))
                for t in range(TPC):
                    ins = pe.transpose(ps[0:E, BANK_A, t * (P // 2):(t + 1) * (P // 2)].bitcast(F16), gate16[:, t, :],
                                       ident16[:, :])
                ins.then_inc(gatet_psum, 1)

            def gates_b2(j):
                pe.wait_ge(gatet_ready, j + 1)
                for t in range(TPC):
                    rows = slice(t * P, (t + 1) * P)
                    pe.matmul(ps[:, BANK_A, rows], gate_t[:, rows], b2_pair[:, 0, :], start=True, stop=False)
                    ins = pe.matmul(ps[:, BANK_A, rows], gate_t[:, rows], b2_pair[:, 1, :], start=False, stop=True)
                ins.then_inc(b2_psum, 1)

            def up(j, par, e, early=False):
                if early and e == 0:
                    pe.wait_ge(gate_chain, 1)
                    pe.wait_ge(pt_by_dve, len(DVE_GROUPS) * HEADS * NT)
                for b in range(HB):
                    slot = (2 * e + b) % UP_BANKS
                    if not (early and e < UP_BANKS // HB):
                        pe.wait_ge(hid_raw_ready, 16 * j + 2 * e + b - 3)
                    cols = slice((HB * e + b) * P, (HB * e + b + 1) * P)
                    pe.matmul(ps[:, slot, :], w1_pair[:, 0, cols], x2t_hi[:, par, :], start=True, stop=False)
                    pe.matmul(ps[:, slot, :], w1_pair[:, 0, cols], x2t_lo[:, par, :], start=False, stop=False)
                    pe.matmul(ps[:, slot, :], w1_pair[:, 1, cols], x2t_hi[:, par, :], start=False,
                              stop=True).then_inc(up_done, 1)

            def down(j, e, early=False):
                pe.wait_ge(hid_lo_ready, 16 * j + 2 * e + 2)
                if not (early and e < 2):
                    pe.wait_ge(combined, 8 * j + e - 1)
                elif e == 0:
                    pe.wait_ge(sat_ready, 2 * NT)
                for t in range(TPC):
                    bank = ps[:, AV0 + e % 2, t * D:(t + 1) * D]
                    for b in range(HB):
                        slot = (2 * e + b) % HID_RING
                        rows = slice(t * P, (t + 1) * P)
                        cols = slice((HB * e + b) * D, (HB * e + b + 1) * D)
                        pe.matmul(bank, hid_hi[:, slot, rows], w2_pair[:, 0, cols], start=(b == 0), stop=False)
                        pe.matmul(bank, hid_hi[:, slot, rows], w2_pair[:, 1, cols], start=False, stop=False)
                        ins = pe.matmul(bank, hid_lo[:, slot, rows], w2_pair[:, 0, cols], start=False, stop=(b == HB - 1))
                ins.then_inc(down_done, 1)

            def ffn(j, par, prep=True, early=False):
                for e in range(E):
                    up(j, par, e, early)
                    if prep and e == 1:
                        sat_transpose(j + 1)
                    if prep and e == (3 if early else 2):
                        out_project(j + 1)
                    if e == 3:
                        gate_transpose(j)
                    if e == 4:
                        gates_b2(j)
                    if e >= DOWN_LAG:
                        down(j, e - DOWN_LAG, early)
                    elif not early:
                        down(j - 1, e + E - DOWN_LAG)
                    if prep and e == 6:
                        x2_transpose(j + 1)
                if prep:
                    logits(j + 1, 1 - par)

            ffn(0, 0, early=True)
            ffn(1, 1)
            pairs(pe, 2, NC - 2, ffn)
            ffn(NC - 2, 0)
            ffn(NC - 1, 1, prep=False)
            for e in range(E - DOWN_LAG, E):
                down(NC - 1, e)


INPUTS = ["x", "adj", "L0_gnn_Wq", "L0_gnn_Wk", "L0_gnn_Wv", "L0_gnn_weightr", "L0_gnn_weightd", "L0_gnn_bias",
          "L0_ffn_Wg", "L0_ffn_bg", "L0_ffn_W1", "L0_ffn_b1", "L0_ffn_W2", "L0_ffn_b2"]


def kernel(**inputs):
    import numpy as np
    import concourse.bacc as bacc
    from concourse.bass_utils import run_bass_kernel_spmd

    nc = bacc.Bacc("TRN2", target_bir_lowering=False, num_devices=1)
    arrays, aps = {}, []
    for name in INPUTS:
        a = np.ascontiguousarray(inputs[name])
        arrays[f"in_{name}"] = a
        aps.append(nc.dram_tensor(f"in_{name}", a.shape, mybir.dt.from_np(a.dtype), kind="ExternalInput").ap())
    aps.append(nc.dram_tensor("out", (N, D), F32, kind="ExternalOutput").ap())
    build(nc, *aps)
    r = run_bass_kernel_spmd(nc, [arrays], core_ids=[0])
    return r.results[0]["out"]
```
